# Optimizing a Trainium2 kernel written in Bass

```python
import numpy as np
import jax
import jax.numpy as jnp

def _softmax(x, axis=-1):
    return jax.nn.softmax(x, axis=axis)

def _gelu(x):
    return jax.nn.gelu(x, approximate=True)

def _silu(x):
    return jax.nn.silu(x)

def _sigmoid(x):
    return jax.nn.sigmoid(x)

def _layernorm(x, axis=-1, eps=1e-05):
    m = jnp.mean(x, axis=axis, keepdims=True)
    v = jnp.var(x, axis=axis, keepdims=True)
    return (x - m) / jnp.sqrt(v + eps)

def _scatter_add(tgt, idx, src, axis=0):
    return tgt.at[idx].add(src)

def _segment_sum(src, seg, n):
    return jax.ops.segment_sum(src, seg, n)
kernel_name = 'mk_gnn_preln_d2_gnn_r8_674198'

def setup_inputs(seed: int=0):
    np.random.seed(seed)
    _w = jnp.asarray

    def _rec_inputs():
        import jax
        import jax.numpy as jnp
        _gk = jax.random.key(seed)
        x = -0.000202 + 1 * jax.random.normal(jax.random.fold_in(_gk, 1), (12500, 64), jnp.float32)
        src = jax.random.randint(jax.random.fold_in(_gk, 2), (200000,), 0, 12500, jnp.int32)
        dst = jax.random.randint(jax.random.fold_in(_gk, 3), (200000,), 0, 12500, jnp.int32)
        _o = jnp.argsort(dst, stable=True)
        src = src[_o]
        dst = dst[_o]
        edge_attr_2 = jax.random.uniform(jax.random.fold_in(_gk, 11), (200000, 2), jnp.float32, 0.0, 1)
        edge_type_8 = jax.random.randint(jax.random.fold_in(_gk, 13), (200000,), 0, 8, jnp.int32)
        return (x, src, dst, edge_attr_2, edge_type_8)
    x, src, dst, edge_attr_2, edge_type_8 = _rec_inputs()

    def _L0_gnn_setup():
        import jax, jax.numpy as jnp
        import numpy as np
        N_NODES = 12500
        N_EDGES = 200000
        IN_CH = 64
        OUT_CH = 64
        NUM_K = 9

        def _quad_basis(v):
            return jnp.stack([0.5 * v * v - v + 0.5, -v * v + v + 0.5, 0.5 * v * v], axis=-1)

        def spline_conv(x, src, dst, pseudo, W, root, bias, n_nodes):
            b0 = _quad_basis(pseudo[:, 0])
            b1 = _quad_basis(pseudo[:, 1])
            B = (b0[:, :, None] * b1[:, None, :]).reshape(pseudo.shape[0], NUM_K)
            x_src = x[src]
            msg = B[:, 0:1] * (x_src @ W[0])
            for k in range(1, NUM_K):
                msg = msg + B[:, k:k + 1] * (x_src @ W[k])
            out = jax.ops.segment_sum(msg, dst, num_segments=n_nodes)
            return out + x @ root + bias
        key = jax.random.key(seed)
        ks = jax.random.split(key, 10)
        x = jax.random.normal(ks[0], (N_NODES, IN_CH), dtype=jnp.float32)
        edge_index = jax.random.randint(ks[1], (2, N_EDGES), 0, N_NODES, dtype=jnp.int64)
        pseudo = jax.random.uniform(ks[2], (N_EDGES, 2), dtype=jnp.float32)
        s1 = 1.0 / np.sqrt(IN_CH * NUM_K)
        s2 = 1.0 / np.sqrt(OUT_CH * NUM_K)
        W1 = jax.random.normal(ks[3], (NUM_K, IN_CH, OUT_CH), dtype=jnp.float32) * s1
        root1 = jax.random.normal(ks[4], (IN_CH, OUT_CH), dtype=jnp.float32) * s1
        b1 = jax.random.normal(ks[5], (OUT_CH,), dtype=jnp.float32) * 0.01
        W2 = jax.random.normal(ks[6], (NUM_K, OUT_CH, OUT_CH), dtype=jnp.float32) * s2
        root2 = jax.random.normal(ks[7], (OUT_CH, OUT_CH), dtype=jnp.float32) * s2
        b2 = jax.random.normal(ks[8], (OUT_CH,), dtype=jnp.float32) * 0.01
        return {'x': x, 'edge_index': edge_index, 'pseudo': pseudo, 'W1': W1, 'root1': root1, 'b1': b1, 'W2': W2, 'root2': root2, 'b2': b2}
    _L0_gnn_all = _L0_gnn_setup()
    _L0_gnn_in = {k: v for k, v in _L0_gnn_all.items() if k in ('W1', 'root1', 'b1', 'W2', 'root2', 'b2')}
    del _L0_gnn_all

    def _L1_gnn_setup():
        import jax, jax.numpy as jnp
        import numpy as np
        N_NODES = 6250
        N_EDGES = 200000
        D = 64
        R = 8

        def _rgcn_layer(x, edge_index, edge_type, W, root, bias):
            src, dst = (edge_index[0], edge_index[1])
            h = jnp.einsum('nd,rdf->rnf', x, W)
            msg = h[edge_type, src]
            agg = jax.ops.segment_sum(msg, dst, num_segments=x.shape[0])
            return agg + x @ root + bias
        key = jax.random.key(seed)
        ks = jax.random.split(key, 9)
        adj = jax.random.randint(ks[0], (2, N_EDGES), 0, N_NODES, dtype=jnp.int32)
        features = jax.random.normal(ks[1], (N_NODES, D), dtype=jnp.float32)
        edge_type = jax.random.randint(ks[2], (N_EDGES,), 0, R, dtype=jnp.int32)
        s = 1.0 / np.sqrt(D)
        W1 = jax.random.normal(ks[3], (R, D, D), dtype=jnp.float32) * s
        root1 = jax.random.normal(ks[4], (D, D), dtype=jnp.float32) * s
        b1 = jnp.zeros((D,), dtype=jnp.float32)
        W2 = jax.random.normal(ks[5], (R, D, D), dtype=jnp.float32) * s
        root2 = jax.random.normal(ks[6], (D, D), dtype=jnp.float32) * s
        b2 = jnp.zeros((D,), dtype=jnp.float32)
        return {'adj': adj, 'features': features, 'edge_type': edge_type, 'W1': W1, 'root1': root1, 'b1': b1, 'W2': W2, 'root2': root2, 'b2': b2}
    _L1_gnn_all = _L1_gnn_setup()
    _L1_gnn_in = {k: v for k, v in _L1_gnn_all.items() if k in ('W1', 'root1', 'b1', 'W2', 'root2', 'b2')}
    del _L1_gnn_all
    return {'x': x, 'src': src, 'dst': dst, 'edge_attr_2': edge_attr_2, 'edge_type_8': edge_type_8, 'L0_gnn_W1': _L0_gnn_in['W1'], 'L0_gnn_root1': _L0_gnn_in['root1'], 'L0_gnn_b1': _L0_gnn_in['b1'], 'L0_gnn_W2': _L0_gnn_in['W2'], 'L0_gnn_root2': _L0_gnn_in['root2'], 'L0_gnn_b2': _L0_gnn_in['b2'], 'L1_gnn_W1': _L1_gnn_in['W1'], 'L1_gnn_root1': _L1_gnn_in['root1'], 'L1_gnn_b1': _L1_gnn_in['b1'], 'L1_gnn_W2': _L1_gnn_in['W2'], 'L1_gnn_root2': _L1_gnn_in['root2'], 'L1_gnn_b2': _L1_gnn_in['b2']}

def reference(x, src, dst, edge_attr_2, edge_type_8, L0_gnn_W1, L0_gnn_root1, L0_gnn_b1, L0_gnn_W2, L0_gnn_root2, L0_gnn_b2, L1_gnn_W1, L1_gnn_root1, L1_gnn_b1, L1_gnn_W2, L1_gnn_root2, L1_gnn_b2):
    import jax
    import jax.numpy as jnp

    def _L0_gnn_ref(x, edge_index, pseudo, W1, root1, b1, W2, root2, b2):
        import jax, jax.numpy as jnp
        import numpy as np
        N_NODES = 12500
        N_EDGES = 200000
        IN_CH = 64
        OUT_CH = 64
        NUM_K = 9

        def _quad_basis(v):
            return jnp.stack([0.5 * v * v - v + 0.5, -v * v + v + 0.5, 0.5 * v * v], axis=-1)

        def spline_conv(x, src, dst, pseudo, W, root, bias, n_nodes):
            b0 = _quad_basis(pseudo[:, 0])
            b1 = _quad_basis(pseudo[:, 1])
            B = (b0[:, :, None] * b1[:, None, :]).reshape(pseudo.shape[0], NUM_K)
            x_src = x[src]
            msg = B[:, 0:1] * (x_src @ W[0])
            for k in range(1, NUM_K):
                msg = msg + B[:, k:k + 1] * (x_src @ W[k])
            out = jax.ops.segment_sum(msg, dst, num_segments=n_nodes)
            return out + x @ root + bias
        src, dst = (edge_index[0], edge_index[1])
        h = jax.nn.relu(spline_conv(x, src, dst, pseudo, W1, root1, b1, N_NODES))
        h = jax.nn.relu(spline_conv(h, src, dst, pseudo, W2, root2, b2, N_NODES))
        return h

    def _L1_gnn_ref(adj, features, edge_type, W1, root1, b1, W2, root2, b2):
        import jax, jax.numpy as jnp
        import numpy as np
        N_NODES = 6250
        N_EDGES = 200000
        D = 64
        R = 8

        def _rgcn_layer(x, edge_index, edge_type, W, root, bias):
            src, dst = (edge_index[0], edge_index[1])
            h = jnp.einsum('nd,rdf->rnf', x, W)
            msg = h[edge_type, src]
            agg = jax.ops.segment_sum(msg, dst, num_segments=x.shape[0])
            return agg + x @ root + bias
        x = _rgcn_layer(features, adj, edge_type, W1, root1, b1)
        x = jax.nn.relu(x)
        x = _rgcn_layer(x, adj, edge_type, W2, root2, b2)
        return x
    edge_index = jnp.stack([src, dst])
    h = jnp.maximum(_layernorm(x, axis=-1), 0.0)
    x = x + _L0_gnn_ref(h, edge_index, edge_attr_2, L0_gnn_W1, L0_gnn_root1, L0_gnn_b1, L0_gnn_W2, L0_gnn_root2, L0_gnn_b2)
    h = jnp.maximum(_layernorm(x, axis=-1), 0.0)
    x = x + _L1_gnn_ref(edge_index, h, edge_type_8, L1_gnn_W1, L1_gnn_root1, L1_gnn_b1, L1_gnn_W2, L1_gnn_root2, L1_gnn_b2)
    return x

_drawn_inputs = setup_inputs


def setup_inputs(seed=0):
    import zlib

    import numpy as np

    out = dict(_drawn_inputs(seed))
    spreads = {'L1_gnn_b1': (0.0, 0.456), 'L1_gnn_b2': (0.0, 0.8)}
    factors = {'L0_gnn_b1': 8.0, 'L0_gnn_b2': 8.0}
    for name, (base, spread) in spreads.items():
        noise = np.random.default_rng([zlib.crc32(name.encode()), seed]).standard_normal(out[name].shape)
        drawn = base * np.exp(spread * noise) if base else spread * noise
        out[name] = jnp.asarray(drawn.astype(out[name].dtype))
    for name, factor in factors.items():
        out[name] = (out[name] * factor).astype(out[name].dtype)
    return out
```

```python
from contextlib import ExitStack

import concourse.bass as bass
from concourse import mybir

FP32 = mybir.dt.float32
INT32 = mybir.dt.int32
ALU = mybir.AluOpType
ACT = mybir.ActivationFunctionType
AX = mybir.AxisListType

NODES, EDGES, D = 12500, 200000, 64
P = 128
WINDOW = 128
ROWS = -(-NODES // P)
NODES_UP = ROWS * P
GROUP = 14
CHUNK = 2
CHUNKS = GROUP // CHUNK
GROUPS = -(-EDGES // (P * GROUP))
PAIRS = GROUPS // 2
TILES = GROUPS * GROUP
ACC_ROWS = NODES_UP + WINDOW
SPLINE_K, RELATIONS = 9, 8
LAYER_K = [SPLINE_K, SPLINE_K, RELATIONS, RELATIONS]
LAYERS = len(LAYER_K)
LAST_N = 1 << 17
MAX_PASSES = -(-(NODES + 1) // WINDOW)
HALVES = [(0, 48), (48, ROWS)]
BATCH = 8
BATCHES = -(-ROWS // BATCH)
EPS = 1e-5
MUL, ADD, SUB, MAX = ALU.mult, ALU.add, ALU.subtract, ALU.max
assert GROUPS % 2 == 0 and GROUP % CHUNK == 0


def gnn_kernel(nc, x, src, dst, attr, etype, weights, roots, biases, out):
    ctx = ExitStack()
    with ctx:
        def sb(name, shape, dt=FP32):
            return ctx.enter_context(nc.sbuf_tensor(name, shape, dt))

        def sem(name):
            return ctx.enter_context(nc.semaphore(name))

        table = [nc.dram_tensor(f"table{l}", (NODES_UP, D), FP32, kind="Internal").ap() for l in range(LAYERS)]
        acc = [nc.dram_tensor(f"acc{l}", (ACC_ROWS, D), FP32, kind="Internal").ap() for l in range(LAYERS)]

        xres = sb("xres", [P, ROWS, D])
        h = sb("h", [P, ROWS, D])
        coef = sb("coef", [P, TILES, SPLINE_K])
        rel = sb("rel", [P, TILES])
        srcs = sb("srcs", [P, TILES + 2 * GROUP], INT32)
        etypes = sb("etypes", [P, TILES], INT32)
        rows = sb("rows", [P, 2, GROUP, D])
        index = sb("index", [P, 2, GROUP], INT32)
        relq = sb("relq", [P, GROUP])
        S = sb("S", [P, GROUP, WINDOW])
        M = sb("M", [P, GROUP, SPLINE_K * D])
        A_sb = sb("A_sb", [P, SPLINE_K * D])
        AT_sb = sb("AT_sb", [P, 5, P])
        acc_in = sb("acc_in", [P, D])
        acc_sum = sb("acc_sum", [P, D])
        flat = M[:, :, :].rearrange("p t n -> p (t n)")
        attr_sb = flat[:, 0:2 * TILES].rearrange("p (a t) -> p a t", a=2)
        dst_sb = flat[:, 2 * TILES:3 * TILES].bitcast(INT32)
        squares = flat[:, 3 * TILES:3 * TILES + (ROWS - 48) * D]
        S_flat = S[:, :, :].rearrange("p t n -> p (t n)")
        basis = [[attr_sb[:, 0, :], flat[:, 2 * TILES:3 * TILES], flat[:, 3 * TILES:4 * TILES]],
                 [attr_sb[:, 1, :], S_flat[:, 0:TILES], flat[:, 4 * TILES:5 * TILES]]]
        acc_init = flat[:, 0:ROWS * D].rearrange("p (r f) -> p r f", f=D)
        hT_sb = sb("hT_sb", [P, 2, 4 * P])
        W_sb = [sb(f"W{l}", [P, 5, D]) for l in range(LAYERS)]
        root_sb = [sb(f"root{l}", [P, 2 * D]) for l in range(LAYERS)]
        bias_sb = [sb(f"bias{l}", [P, D]) for l in range(LAYERS)]
        ident = sb("ident", [P, P])
        node_i = sb("node_i", [P, WINDOW], INT32)
        node = sb("node", [P, WINDOW])
        eps = sb("eps", [P, 1])
        zeros = sb("zeros", [P, D])
        least = sb("least", [P, 2, GROUPS])
        ends = sb("ends", [GROUPS, 2])
        ends_wide = sb("ends_wide", [GROUPS, 2, P])
        ends_i = sb("ends_i", [1, 2, GROUPS], INT32)
        span = sb("span", [1, GROUPS])
        tab = sb("tab", [1, GROUPS, 2], INT32)
        mean = sb("mean", [P, ROWS])
        var = sb("var", [P, ROWS])
        std = sb("std", [P, ROWS])

        A = ctx.enter_context(nc.psum_tensor("A", [P, 2, 1024], FP32))
        AT = ctx.enter_context(nc.psum_tensor("AT", [P, 2, 512], FP32))
        O = ctx.enter_context(nc.psum_tensor("O", [P, 2, 512], FP32))

        s_x = [sem(f"s_x{i}") for i in range(2)]
        s_acc_back = [sem(f"s_acc_back{i}") for i in range(2)]
        s_edges = [sem(f"s_edges_{n}") for n in ("src", "dst", "attr", "type")]
        s_weights = sem("s_weights")
        s_root_zero = sem("s_root_zero")
        s_const = sem("s_const")
        s_pool = sem("s_pool")
        s_node = sem("s_node")
        s_v = sem("s_v")
        s_centred = sem("s_centred")
        s_squares = sem("s_squares")
        s_squares_used = sem("s_squares_used")
        s_var = sem("s_var")
        s_std = sem("s_std")
        s_h = sem("s_h")
        s_table = sem("s_table")
        s_hT = sem("s_hT")
        s_hT_sb = sem("s_hT_sb")
        s_root = sem("s_root")
        s_init = sem("s_init")
        s_acc_init = sem("s_acc_init")
        s_tab_min = sem("s_tab_min")
        s_tab_T = sem("s_tab_T")
        s_tab_ends = sem("s_tab_ends")
        s_tab_wide = sem("s_tab_wide")
        s_tab = sem("s_tab")
        s_index = sem("s_index")
        s_gathered = [[sem(f"s_gathered{a}_{c}") for c in range(CHUNKS)] for a in range(2)]
        s_rel = sem("s_rel")
        s_vec_chunk = sem("s_vec_chunk")
        s_act_chunk = sem("s_act_chunk")
        s_chunk_free = sem("s_chunk_free")
        s_A_sb = sem("s_A_sb")
        s_AT = sem("s_AT")
        s_AT_sb = sem("s_AT_sb")
        s_O = sem("s_O")
        s_sum = sem("s_sum")
        s_acc_load = sem("s_acc_load")
        s_acc_store = sem("s_acc_store")
        s_out = sem("s_out")

        block = ctx.enter_context(nc.Block())

        def node_view(dram, a, b):
            return dram[0:NODES_UP, :].rearrange("(p r) f -> p r f", r=ROWS)[:, a:b, :]

        def counter(eng, name):
            reg = eng.alloc_register(name)
            eng.reg_mov(reg, 0)
            return reg

        @block.sync
        def _(eng):
            for i, (a, b) in enumerate(HALVES):
                eng.dma_start(xres[:, a:b, :], node_view(x, a, b)).then_inc(s_x[i], 16)
            eng.dma_start(srcs[:, 0:TILES], src).then_inc(s_edges[0], 16)
            eng.dma_start(srcs[:, TILES:], src[:, 0:2 * GROUP]).then_inc(s_edges[0], 16)
            eng.dma_start(dst_sb, dst).then_inc(s_edges[1], 16)
            eng.dma_start(attr_sb, attr).then_inc(s_edges[2], 16)
            eng.dma_start(etypes[:, :], etype).then_inc(s_edges[3], 16)

            passes = counter(eng, "sync_passes")
            first_row = counter(eng, "sync_first_row")
            stores = counter(eng, "sync_stores")
            sums = counter(eng, "sync_sums")
            for l in range(LAYERS):
                for i, (a, b) in enumerate(HALVES):
                    eng.wait_ge(s_h, 2 * l + i + 1)
                    eng.dma_start(node_view(table[l], a, b), h[:, a:b, :]).then_inc(s_table, 16)
                eng.wait_ge(s_init, BATCHES * (l + 1))
                eng.dma_start(node_view(acc[l], 0, ROWS), acc_init).then_inc(s_acc_init, 16)
                eng.dma_start(acc[l][NODES_UP:ACC_ROWS, :], zeros[:, :]).then_inc(s_acc_init, 16)
                eng.wait_ge(s_acc_init, 32 * (l + 1))
                if l == 0:
                    eng.wait_ge(s_tab, 1)
                with eng.Fori(0, GROUPS) as g:
                    start = eng.value_load(tab[0:1, bass.ds(g, 1), 0:1].rearrange("p a b -> p (a b)"),
                                           min_val=0, max_val=NODES)
                    count = eng.value_load(tab[0:1, bass.ds(g, 1), 1:2].rearrange("p a b -> p (a b)"),
                                           min_val=1, max_val=MAX_PASSES)
                    eng.reg_mov(first_row, start)
                    with eng.Fori(0, count):
                        n = eng.snap(passes, min_val=0, max_val=LAST_N)
                        window = acc[l][bass.ds(eng.snap(first_row, min_val=0, max_val=NODES), WINDOW), :]
                        eng.reg_mov(stores, n * 16)
                        eng.reg_mov(sums, n + (l + 1))
                        eng.wait_ge(s_acc_store, stores)
                        eng.wait_ge(s_sum, sums)
                        eng.dma_start(acc_in[:, :], window).then_inc(s_acc_load, 16)
                        eng.wait_ge(s_sum, n + (l + 2))
                        eng.dma_start(window, acc_sum[:, :]).then_inc(s_acc_store, 16)
                        eng.reg_add(passes, passes, 1)
                        eng.reg_add(first_row, first_row, WINDOW)
                stored = eng.snap(eng.snap(passes, min_val=0, max_val=LAST_N) * 16)
                eng.wait_ge(s_acc_store, stored)
                eng.wait_ge(s_table, 32 * (l + 1))
                eng.wait_ge(s_root, BATCHES * (l + 1))
                for i, (a, b) in enumerate(HALVES):
                    eng.dma_start(h[:, a:b, :], node_view(acc[l], a, b)).then_inc(s_acc_back[i], 16)
            for i, (a, b) in enumerate(HALVES):
                eng.wait_ge(s_h, 2 * LAYERS + i + 1)
                eng.dma_start(node_view(out, a, b), h[:, a:b, :]).then_inc(s_out, 16)
            eng.wait_ge(s_out, 32)

        @block.gpsimd
        def _(eng):
            eng.memset(ident[:, :], 0.0).then_inc(s_pool, 1)
            eng.wait_ge(s_pool, 1)
            eng.affine_select(out=ident[:, :], in_=ident[:, :], compare_op=ALU.not_equal, fill=1.0,
                              base=0, pattern=[[-1, P]], channel_multiplier=1).then_inc(s_const, 1)
            eng.iota(node_i[:, :], pattern=[[1, WINDOW]], base=0, channel_multiplier=0).then_inc(s_const, 1)
            groups = counter(eng, "gpsimd_groups")
            for l in range(LAYERS):
                eng.wait_ge(s_table, 32 * (l + 1))
                with eng.Fori(0, PAIRS):
                    for side in range(2):
                        group = eng.snap(groups, min_val=0, max_val=LAYERS * GROUPS)
                        eng.wait_ge(s_index, group + 1)
                        eng.reg_add(groups, groups, 1)
                        for t in range(GROUP):
                            eng.indirect_dma_start(
                                rows[:, side, t, :], None, table[l],
                                bass.IndirectOffsetOnAxis(ap=index[:, side, t:t + 1], axis=0),
                            ).then_inc(s_gathered[side][t // CHUNK], 16)

        @block.scalar
        def _(eng):
            eng.wait_ge(s_root_zero, 1)
            for l in range(LAYERS):
                full, rest = divmod(LAYER_K[l] * D, P)
                eng.dma_start(root_sb[l][0:D, 0:D], roots[l]).then_inc(s_weights, 16)
                eng.dma_start(root_sb[l][D:P, D:2 * D], roots[l]).then_inc(s_weights, 16)
                eng.dma_start(bias_sb[l][:, :], biases[l].rearrange("(a f) -> a f", a=1).to_broadcast([P, D]))\
                   .then_inc(s_weights, 16)
                eng.dma_start(W_sb[l][:, 0:full, :],
                              weights[l][0:full * P, :].rearrange("(c p) f -> p c f", p=P)).then_inc(s_weights, 16)
                if rest:
                    eng.dma_start(W_sb[l][0:rest, full, :], weights[l][full * P:, :]).then_inc(s_weights, 16)

            def norm(done):
                for i, (a, b) in enumerate(HALVES):
                    eng.wait_ge(s_centred, 2 * done + i + 1)
                    if i or done:
                        eng.wait_ge(s_squares_used, 2 * done + i)
                    eng.activation(squares[:, 0:(b - a) * D], h[:, a:b, :].rearrange("p r f -> p (r f)"),
                                   ACT.Square).then_inc(s_squares, 1)
                for i, (a, b) in enumerate(HALVES):
                    eng.wait_ge(s_var, 2 * done + i + 1)
                    eng.activation(std[:, a:b], var[:, a:b], ACT.Sqrt, bias=eps[:, 0:1], scale=1.0 / D)\
                       .then_inc(s_std, 1)

            def evacuate_A(l, n):
                eng.wait_ge(s_chunk_free, n * CHUNKS + CHUNKS)
                eng.wait_ge(s_AT, n + l)
                eng.activation(A_sb[:, 0:LAYER_K[l] * D].unsqueeze(1),
                               A[:, bass.ds((n + 1) % 2, 1), 0:LAYER_K[l] * D], ACT.Copy).then_inc(s_A_sb, 1)

            def evacuate_AT(l, n):
                full, rest = divmod(LAYER_K[l] * D, P)
                eng.wait_ge(s_AT, n + (l + 1))
                eng.wait_ge(s_O, n + l)
                last = eng.activation(AT_sb[:, 0:full, :].rearrange("p c n -> p (c n)"),
                                      AT[:, 0, 0:full * P], ACT.Copy)
                if rest:
                    last = eng.activation(AT_sb[0:rest, full, :], AT[0:rest, 1, 0:P], ACT.Copy)
                last.then_inc(s_AT_sb, 1)

            eng.wait_ge(s_node, 1)
            passes = counter(eng, "scalar_passes")
            for l in range(LAYERS):
                if l in (0, 2):
                    norm(l // 2)
                for b in range(BATCHES):
                    eng.wait_ge(s_hT, l * BATCHES + b + 1)
                    if b >= 2:
                        eng.wait_ge(s_root, l * BATCHES + b - 1)
                    w = min(BATCH, ROWS - b * BATCH) * D
                    eng.activation(hT_sb[:, b % 2, 0:w], AT[:, b % 2, 0:w], ACT.Copy).then_inc(s_hT_sb, 1)
                if l == 0:
                    eng.wait_ge(s_tab, 1)
                if l in (0, 2):
                    eng.wait_ge(s_tab, 2 + l // 2)
                eng.wait_ge(s_acc_init, 32 * (l + 1))
                k = LAYER_K[l] - 1
                with eng.Fori(0, PAIRS) as pair:
                    for side in range(2):
                        g = eng.snap(pair * 2 + side, min_val=0, max_val=GROUPS - 1)
                        count = eng.value_load(tab[0:1, bass.ds(g, 1), 1:2].rearrange("p a b -> p (a b)"),
                                               min_val=1, max_val=MAX_PASSES)
                        tile0 = eng.snap(g * GROUP, min_val=0, max_val=TILES - GROUP)
                        with eng.Fori(0, count):
                            n = eng.snap(passes, min_val=0, max_val=LAST_N)
                            for c in range(CHUNKS):
                                eng.wait_ge(s_gathered[side][c], pair * (16 * CHUNK) + 16 * CHUNK * (l * PAIRS + 1))
                                eng.wait_ge(s_chunk_free, n * CHUNKS + (c + 1))
                                for t in range(c * CHUNK, (c + 1) * CHUNK):
                                    eng.activation(M[:, t, k * D:(k + 1) * D], rows[:, side, t, :], ACT.Copy,
                                                   scale=coef[:, bass.ds(tile0 + t, 1), k:k + 1]
                                                   .rearrange("p a b -> p (a b)")).then_inc(s_act_chunk, 1)
                                if c == 1:
                                    evacuate_A(l, n)
                                if c == 3:
                                    evacuate_AT(l, n)
                            eng.reg_add(passes, passes, 1)
                n = eng.snap(passes, min_val=0, max_val=LAST_N)
                evacuate_A(l, n)
                evacuate_AT(l, n)

        @block.tensor
        def _(eng):
            eng.wait_ge(s_const, 2)
            eng.wait_ge(s_node, 1)

            def transpose_batch(l, b):
                half = 0 if (b + 1) * BATCH <= HALVES[0][1] else 1
                eng.wait_ge(s_h, 2 * l + half + 1)
                if b >= 2:
                    eng.wait_ge(s_hT_sb, l * BATCHES + b - 1)
                n = min(BATCH, ROWS - b * BATCH) // 2
                for t in range(n):
                    r = b * BATCH + 2 * t
                    last = eng.transpose(AT[:, b % 2, t * P:(t + 1) * P],
                                         h[:, r:r + 2, :].rearrange("p r f -> p (r f)"), ident[:, :])
                last.then_inc(s_hT, 1)

            def root_batch(l, b):
                eng.wait_ge(s_hT_sb, l * BATCHES + b + 1)
                if b >= 2:
                    eng.wait_ge(s_init, l * BATCHES + b - 1)
                n = min(BATCH, ROWS - b * BATCH) // 2
                for t in range(n):
                    last = eng.matmul(O[:, b % 2, t * 2 * D:(t + 1) * 2 * D], hT_sb[:, b % 2, t * P:(t + 1) * P],
                                      root_sb[l][:, :], start=True, stop=True)
                last.then_inc(s_root, 1)

            def group_tables():
                eng.wait_ge(s_tab_min, 1)
                for i in range(2):
                    last = eng.transpose(AT[0:GROUPS, 0, i * P:(i + 1) * P], least[:, i, :], ident[:, :])
                last.then_inc(s_tab_T, 1)
                eng.wait_ge(s_tab_ends, 1)
                for i in range(2):
                    last = eng.matmul(O[:, 0, i * P:i * P + GROUPS], ends_wide[:, i, :], ident[0:GROUPS, 0:GROUPS],
                                      start=True, stop=True)
                last.then_inc(s_tab_wide, 1)

            def transpose_A(l, n):
                full, rest = divmod(LAYER_K[l] * D, P)
                eng.wait_ge(s_A_sb, n + (l + 1))
                eng.wait_ge(s_AT_sb, n + l)
                for c in range(full):
                    last = eng.transpose(AT[:, 0, c * P:(c + 1) * P], A_sb[:, c * P:(c + 1) * P], ident[:, :])
                if rest:
                    last = eng.transpose(AT[0:rest, 1, 0:P], A_sb[:, full * P:full * P + rest], ident[:, :])
                last.then_inc(s_AT, 1)

            def project(l, n):
                full, rest = divmod(LAYER_K[l] * D, P)
                eng.wait_ge(s_AT_sb, n + (l + 1))
                eng.wait_ge(s_sum, n + l)
                for c in range(full):
                    last = eng.matmul(O[:, 0, 0:D], AT_sb[:, c, :], W_sb[l][:, c, :],
                                      start=(c == 0), stop=(c == full - 1 and not rest))
                if rest:
                    last = eng.matmul(O[:, 0, 0:D], AT_sb[0:rest, full, :], W_sb[l][0:rest, full, :],
                                      start=False, stop=True)
                last.then_inc(s_O, 1)

            passes = counter(eng, "tensor_passes")
            for l in range(LAYERS):
                if l == 0:
                    group_tables()
                    eng.wait_ge(s_tab, 1)
                    eng.wait_ge(s_weights, 16 * sum(4 + (k * D % P > 0) for k in LAYER_K))
                    eng.sem_inc(s_chunk_free, CHUNKS)
                transpose_batch(l, 0)
                for b in range(BATCHES):
                    if b + 1 < BATCHES:
                        transpose_batch(l, b + 1)
                    root_batch(l, b)
                width = LAYER_K[l] * D
                with eng.Fori(0, PAIRS) as pair:
                    for side in range(2):
                        count = eng.value_load(tab[0:1, bass.ds(pair * 2 + side, 1), 1:2]
                                               .rearrange("p a b -> p (a b)"), min_val=1, max_val=MAX_PASSES)
                        with eng.Fori(0, count):
                            n = eng.snap(passes, min_val=0, max_val=LAST_N)
                            buf = eng.snap(n % 2, min_val=0, max_val=1)
                            eng.wait_ge(s_A_sb, n + l)
                            for c in range(CHUNKS):
                                eng.wait_ge(s_vec_chunk, n * CHUNKS + (c + 1))
                                eng.wait_ge(s_act_chunk, n * GROUP + CHUNK * (c + 1))
                                for t in range(c * CHUNK, (c + 1) * CHUNK):
                                    for lo in range(0, width, 512):
                                        hi = min(width, lo + 512)
                                        last = eng.matmul(A[:, bass.ds(buf, 1), lo:hi].rearrange("p a n -> p (a n)"),
                                                          S[:, t, :], M[:, t, lo:hi],
                                                          start=(t == 0), stop=(t == GROUP - 1))
                                last.then_inc(s_chunk_free, 1)
                                if c == 1:
                                    transpose_A(l, n)
                                if c == 3:
                                    project(l, n)
                            eng.reg_add(passes, passes, 1)
                n = eng.snap(passes, min_val=0, max_val=LAST_N)
                transpose_A(l, n)
                project(l, n)

        @block.vector
        def _(eng):
            steps = [0]

            def step(ins):
                steps[0] += 1
                ins.then_inc(s_v, 1)

            def settled():
                eng.wait_ge(s_v, steps[0])

            for l in range(LAYERS):
                step(eng.memset(root_sb[l][:, :], 0.0))
            settled()
            eng.memset(eps[:, :], EPS).then_inc(s_root_zero, 1)
            eng.memset(zeros[:, :], 0.0)
            eng.memset(acc_in[:, :], 0.0)
            eng.memset(A[:, :, :], 0.0).then_inc(s_node, 1)
            eng.wait_ge(s_const, 2)
            step(eng.tensor_copy(node[:, :], node_i[:, :]))

            def wide(v, n):
                return v.unsqueeze(2).to_broadcast([P, v.shape[1], n])

            def norm(done):
                for i, (a, b) in enumerate(HALVES):
                    if not done:
                        eng.wait_ge(s_x[i], 16)
                    settled()
                    step(eng.tensor_reduce(mean[:, a:b], xres[:, a:b, :], AX.X, ADD))
                    settled()
                    step(eng.tensor_scalar(mean[:, a:b], mean[:, a:b], 1.0 / D, None, MUL))
                    settled()
                    eng.tensor_tensor(h[:, a:b, :], xres[:, a:b, :], wide(mean[:, a:b], D), SUB)\
                       .then_inc(s_centred, 1)
                for i, (a, b) in enumerate(HALVES):
                    eng.wait_ge(s_squares, 2 * done + i + 1)
                    eng.tensor_reduce(var[:, a:b], squares[:, 0:(b - a) * D].rearrange("p (r f) -> p r f", f=D),
                                      AX.X, ADD).then_inc(s_squares_used, 1)
                    eng.wait_ge(s_squares_used, 2 * done + i + 1)
                    eng.sem_inc(s_var, 1)
                for i, (a, b) in enumerate(HALVES):
                    eng.wait_ge(s_std, 2 * done + i + 1)
                    step(eng.reciprocal(std[:, a:b], std[:, a:b]))
                    settled()
                    eng.scalar_tensor_tensor(out=h[:, a:b, :], in0=h[:, a:b, :], scalar=0.0,
                                             in1=wide(std[:, a:b], D), op0=MAX, op1=MUL).then_inc(s_h, 1)

            def group_tables():
                eng.wait_ge(s_edges[1], 16)
                step(eng.tensor_copy(rel[:, :], dst_sb))
                settled()
                by_group = rel[:, :].rearrange("p (g t) -> p g t", t=GROUP)
                step(eng.tensor_reduce(least[:, 0, :], by_group, AX.X, ALU.min))
                eng.tensor_reduce(least[:, 1, :], by_group, AX.X, MAX).then_inc(s_tab_min, 1)
                eng.wait_ge(s_tab_T, 1)
                step(eng.tensor_reduce(ends[:, 0:1], AT[0:GROUPS, 0, 0:P], AX.X, ALU.min))
                step(eng.tensor_reduce(ends[:, 1:2], AT[0:GROUPS, 0, P:2 * P], AX.X, MAX))
                settled()
                eng.tensor_copy(ends_wide[:, :, :], ends[:, :].unsqueeze(2).to_broadcast([GROUPS, 2, P]))\
                   .then_inc(s_tab_ends, 1)
                eng.wait_ge(s_tab_wide, 1)
                step(eng.tensor_tensor(by_group, by_group,
                                       O[:, 0, 0:GROUPS].unsqueeze(2).to_broadcast([P, GROUPS, GROUP]), SUB))
                step(eng.tensor_copy(ends_i[0:1, :, :],
                                     O[0:1, 0, 0:2 * P].rearrange("p (a g) -> p a g", a=2)[:, :, 0:GROUPS]))
                settled()
                step(eng.tensor_tensor(ends_i[0:1, 1, :], ends_i[0:1, 1, :], ends_i[0:1, 0, :], SUB))
                step(eng.tensor_copy(tab[0:1, :, 0], ends_i[0:1, 0, :]))
                settled()
                step(eng.tensor_scalar(ends_i[0:1, 1, :], ends_i[0:1, 1, :], WINDOW.bit_length() - 1, None,
                                       ALU.arith_shift_right))
                settled()
                step(eng.tensor_scalar(span[0:1, :], ends_i[0:1, 1, :], 1.0, None, ADD))
                settled()
                eng.tensor_copy(tab[0:1, :, 1], span[0:1, :]).then_inc(s_tab, 1)

            def spline_coef():
                eng.wait_ge(s_edges[2], 16)
                for a in range(2):
                    v = attr_sb[:, a, :]
                    step(eng.scalar_tensor_tensor(out=basis[a][2], in0=v, scalar=0.5, in1=v, op0=MUL, op1=MUL))
                    step(eng.scalar_tensor_tensor(out=basis[a][1], in0=v, scalar=-1.0, in1=v, op0=MUL, op1=MUL))
                    settled()
                    step(eng.scalar_tensor_tensor(out=basis[a][1], in0=basis[a][1], scalar=0.5, in1=v,
                                                  op0=ADD, op1=ADD))
                    settled()
                    step(eng.scalar_tensor_tensor(out=basis[a][0], in0=basis[a][2], scalar=0.5, in1=v,
                                                  op0=ADD, op1=SUB))
                settled()
                for i in range(3):
                    for j in range(3):
                        last = eng.tensor_tensor(coef[:, :, 3 * i + j], basis[0][i], basis[1][j], MUL)
                last.then_inc(s_tab, 1)

            def relation_coef():
                eng.wait_ge(s_edges[3], 16)
                for r in range(RELATIONS):
                    last = eng.tensor_scalar(coef[:, :, r], etypes[:, :], float(r), None, ALU.is_equal)
                last.then_inc(s_tab, 1)

            def flush(l, n):
                eng.wait_ge(s_O, n + (l + 1))
                eng.wait_ge(s_acc_load, n * 16)
                eng.tensor_tensor(acc_sum[:, :], O[:, 0, 0:D], acc_in[:, :], ADD).then_inc(s_sum, 1)

            passes = counter(eng, "vector_passes")
            for l in range(LAYERS):
                if l == 0:
                    eng.wait_ge(s_edges[0], 32)
                    for side in range(2):
                        eng.tensor_copy(index[:, side, :], srcs[:, side * GROUP:(side + 1) * GROUP])\
                           .then_inc(s_index, 1)
                    norm(0)
                    group_tables()
                    spline_coef()
                else:
                    for i, (a, b) in enumerate(HALVES):
                        eng.wait_ge(s_acc_back[i], 16 * l)
                        if l in (1, 3):
                            eng.tensor_scalar(h[:, a:b, :], h[:, a:b, :], 0.0, None, MAX).then_inc(s_h, 1)
                        else:
                            step(eng.scalar_tensor_tensor(out=xres[:, a:b, :], in0=h[:, a:b, :], scalar=0.0,
                                                          in1=xres[:, a:b, :], op0=MAX, op1=ADD))
                    if l == 2:
                        norm(1)
                if l == 0:
                    eng.wait_ge(s_tab, 2)
                    eng.wait_ge(s_weights, 16 * sum(4 + (k * D % P > 0) for k in LAYER_K))
                if l == 2:
                    relation_coef()
                for b in range(BATCHES):
                    eng.wait_ge(s_root, l * BATCHES + b + 1)
                    r0, r1 = b * BATCH, min(ROWS, (b + 1) * BATCH)
                    eng.tensor_tensor(acc_init[:, r0:r1, :],
                                      O[:, b % 2, 0:(r1 - r0) * D].rearrange("p (r f) -> p r f", f=D),
                                      bias_sb[l][:, :].unsqueeze(1).to_broadcast([P, r1 - r0, D]), ADD)\
                       .then_inc(s_init, 1)
                eng.wait_ge(s_acc_init, 32 * (l + 1))
                if l in (0, 2):
                    eng.wait_ge(s_tab, 2 + l // 2)
                ks = LAYER_K[l] - 1
                with eng.Fori(0, PAIRS) as pair:
                    for side in range(2):
                        g = eng.snap(pair * 2 + side, min_val=0, max_val=GROUPS - 1)
                        count = eng.value_load(tab[0:1, bass.ds(g, 1), 1:2].rearrange("p a b -> p (a b)"),
                                               min_val=1, max_val=MAX_PASSES)
                        tile0 = eng.snap(g * GROUP, min_val=0, max_val=TILES - GROUP)
                        n = eng.snap(passes, min_val=0, max_val=LAST_N)
                        eng.wait_ge(s_rel, n + g + l * GROUPS)
                        eng.tensor_copy(relq[:, :], rel[:, bass.ds(tile0, GROUP)]).then_inc(s_rel, 1)
                        with eng.Fori(0, count):
                            n = eng.snap(passes, min_val=0, max_val=LAST_N)
                            eng.wait_ge(s_rel, n + g + (l * GROUPS + 1))
                            for c in range(CHUNKS):
                                t0, t1 = c * CHUNK, (c + 1) * CHUNK
                                eng.wait_ge(s_chunk_free, n * CHUNKS + (c + 1))
                                eng.tensor_tensor(S[:, t0:t1, :],
                                                  node[:, :].unsqueeze(1).to_broadcast([P, CHUNK, WINDOW]),
                                                  relq[:, t0:t1].unsqueeze(2).to_broadcast([P, CHUNK, WINDOW]),
                                                  ALU.is_equal)
                                eng.wait_ge(s_gathered[side][c], pair * (16 * CHUNK) + 16 * CHUNK * (l * PAIRS + 1))
                                eng.tensor_tensor(
                                    M[:, t0:t1, 0:ks * D].rearrange("p t (k f) -> p t k f", f=D),
                                    rows[:, side, t0:t1, :].unsqueeze(2).to_broadcast([P, CHUNK, ks, D]),
                                    coef[:, bass.ds(tile0 + t0, CHUNK), 0:ks].unsqueeze(3)
                                    .to_broadcast([P, CHUNK, ks, D]), MUL).then_inc(s_vec_chunk, 1)
                            flush(l, n)
                            eng.wait_ge(s_vec_chunk, n * CHUNKS + CHUNKS)
                            eng.tensor_scalar(relq[:, :], relq[:, :], float(WINDOW), None, SUB).then_inc(s_rel, 1)
                            eng.reg_add(passes, passes, 1)
                        n = eng.snap(passes, min_val=0, max_val=LAST_N)
                        eng.wait_ge(s_act_chunk, n * GROUP)
                        eng.wait_ge(s_vec_chunk, n * CHUNKS)
                        eng.tensor_copy(index[:, side, :], srcs[:, bass.ds(tile0 + 2 * GROUP, GROUP)])\
                           .then_inc(s_index, 1)
                n = eng.snap(passes, min_val=0, max_val=LAST_N)
                flush(l, n)
            for i, (a, b) in enumerate(HALVES):
                eng.wait_ge(s_acc_back[i], 16 * LAYERS)
                eng.tensor_tensor(h[:, a:b, :], xres[:, a:b, :], h[:, a:b, :], ADD).then_inc(s_h, 1)
    return nc


def kernel(**inputs):
    import numpy as np
    import concourse.bacc as bacc
    from concourse.bass_utils import run_bass_kernel_spmd

    def by_tile(a, fill):
        a = np.asarray(a)
        up = np.full((TILES * P,) + a.shape[1:], fill, a.dtype)
        up[:EDGES] = a
        up = up.reshape((GROUPS, P, GROUP) + a.shape[1:])
        return np.ascontiguousarray(np.moveaxis(up, 1, 0)).reshape((P, TILES) + a.shape[1:])

    x = np.zeros((NODES_UP, D), np.asarray(inputs["x"]).dtype)
    x[:NODES] = inputs["x"]
    arrays = {
        "x": x,
        "src": by_tile(inputs["src"], 0),
        "dst": by_tile(inputs["dst"], NODES),
        "attr": np.ascontiguousarray(np.moveaxis(by_tile(inputs["edge_attr_2"], 0), 2, 1)),
        "etype": by_tile(inputs["edge_type_8"], 0),
    }
    for part in ("L0", "L1"):
        for n in ("1", "2"):
            w = np.asarray(inputs[f"{part}_gnn_W{n}"])
            arrays[f"W_{part}_{n}"] = np.ascontiguousarray(w.reshape(-1, D))
            arrays[f"root_{part}_{n}"] = np.ascontiguousarray(inputs[f"{part}_gnn_root{n}"])
            arrays[f"b_{part}_{n}"] = np.ascontiguousarray(inputs[f"{part}_gnn_b{n}"])

    nc = bacc.Bacc("TRN2", target_bir_lowering=False, num_devices=1)
    aps = {name: nc.dram_tensor(name, a.shape, mybir.dt.from_np(a.dtype), kind="ExternalInput").ap()
           for name, a in arrays.items()}
    out = nc.dram_tensor("out", (NODES_UP, D), FP32, kind="ExternalOutput").ap()
    layers = [f"{part}_{n}" for part in ("L0", "L1") for n in ("1", "2")]
    gnn_kernel(nc, aps["x"], aps["src"], aps["dst"], aps["attr"], aps["etype"],
               [aps["W_" + s] for s in layers], [aps["root_" + s] for s in layers],
               [aps["b_" + s] for s in layers], out)
    got = run_bass_kernel_spmd(nc, [arrays], core_ids=[0])
    return got.results[0]["out"][:NODES]
```

```python
from contextlib import ExitStack

import concourse.bass as bass
from concourse import mybir

FP32 = mybir.dt.float32
INT32 = mybir.dt.int32
ALU = mybir.AluOpType
ACT = mybir.ActivationFunctionType
AX = mybir.AxisListType

NODES, EDGES, D = 12500, 200000, 64
P = 128
WINDOW = 128
ROWS = -(-NODES // P)
NODES_UP = ROWS * P
GROUP = 14
CHUNK = 2
CHUNKS = GROUP // CHUNK
GROUPS = -(-EDGES // (P * GROUP))
PAIRS = GROUPS // 2
TILES = GROUPS * GROUP
ACC_ROWS = NODES_UP + WINDOW
SPLINE_K, RELATIONS = 9, 8
LAYER_K = [SPLINE_K, SPLINE_K, RELATIONS, RELATIONS]
LAYERS = len(LAYER_K)
LAST_N = 1 << 17
MAX_PASSES = -(-(NODES + 1) // WINDOW)
PARTS = [(0, 24), (24, 48), (48, 72), (72, ROWS)]
LONGEST = max(b - a for a, b in PARTS)
BATCH = 8
BATCHES = -(-ROWS // BATCH)
EPS = 1e-5
MUL, ADD, SUB, MAX = ALU.mult, ALU.add, ALU.subtract, ALU.max
BANK = 512
SPLITS = {SPLINE_K: 2, RELATIONS: 1}
assert GROUPS % 2 == 0 and GROUP % CHUNK == 0


def gnn_kernel(nc, x, src, dst, attr, etype, weights, roots, biases, out):
    ctx = ExitStack()
    with ctx:
        def sb(name, shape, dt=FP32):
            return ctx.enter_context(nc.sbuf_tensor(name, shape, dt))

        def sem(name):
            return ctx.enter_context(nc.semaphore(name))

        table = {l: nc.dram_tensor(f"table{l}", (NODES_UP, D), FP32, kind="Internal").ap() for l in (0, 2)}
        acc = [nc.dram_tensor(f"acc{l}", (ACC_ROWS, D), FP32, kind="Internal").ap() for l in range(LAYERS)]

        xres = sb("xres", [P, ROWS, D])
        h = sb("h", [P, ROWS, D])
        basis = sb("basis", [P, 2, TILES, 3])
        rel = sb("rel", [P, TILES])
        srcs = sb("srcs", [P, TILES + 2 * GROUP], INT32)
        relation = sb("relation", [P, TILES])
        rows = sb("rows", [P, 2, GROUP, D])
        index = sb("index", [P, 2, GROUP], INT32)
        coef = sb("coef", [P, GROUP, SPLINE_K])
        relq = sb("relq", [P, GROUP])
        S = sb("S", [P, GROUP, WINDOW])
        M = sb("M", [P, GROUP, SPLINE_K * D])
        A_sb = sb("A_sb", [P, SPLINE_K * D])
        AT_sb = sb("AT_sb", [P, 5, P])
        acc_in = sb("acc_in", [P, D])
        acc_sum = sb("acc_sum", [P, D])
        acc_init = sb("acc_init", [P, ROWS, D])
        flat = M[:, :, :].rearrange("p t n -> p (t n)")
        attr_sb = flat[:, 0:2 * TILES].rearrange("p (a t) -> p a t", a=2)
        etype_sb = flat[:, 2 * TILES:3 * TILES].bitcast(INT32)
        squares = [flat[:, 3 * TILES + i * LONGEST * D:3 * TILES + (i + 1) * LONGEST * D] for i in range(2)]
        dst_sb = acc_init[:, :, :].rearrange("p r f -> p (r f)")[:, 0:TILES].bitcast(INT32)
        hT_sb = sb("hT_sb", [P, 2, 4 * P])
        W_sb = [sb(f"W{l}", [P, 5, D]) for l in range(LAYERS)]
        root_sb = [sb(f"root{l}", [P, 2 * D]) for l in range(LAYERS)]
        bias_sb = [sb(f"bias{l}", [P, D]) for l in range(LAYERS)]
        ident = sb("ident", [P, P])
        node_i = sb("node_i", [P, WINDOW], INT32)
        node = sb("node", [P, WINDOW])
        eps = sb("eps", [P, 1])
        zeros = sb("zeros", [P, D])
        least = sb("least", [P, 2, GROUPS])
        ends = sb("ends", [GROUPS, 2])
        ends_wide = sb("ends_wide", [GROUPS, 2, P])
        ends_i = sb("ends_i", [1, 2, GROUPS], INT32)
        span = sb("span", [1, GROUPS])
        tab = sb("tab", [1, GROUPS, 2], INT32)
        mean = sb("mean", [P, ROWS])
        var = sb("var", [P, ROWS])
        std = sb("std", [P, ROWS])

        A = ctx.enter_context(nc.psum_tensor("A", [P, 2, 1024], FP32))
        AT = ctx.enter_context(nc.psum_tensor("AT", [P, 2, 512], FP32))
        O = ctx.enter_context(nc.psum_tensor("O", [P, 2, 512], FP32))

        s_x = [sem(f"s_x{i}") for i in range(len(PARTS))]
        s_acc_back = [sem(f"s_acc_back{i}") for i in range(len(PARTS))]
        s_edges = [sem(f"s_edges_{n}") for n in ("src", "dst", "attr", "type")]
        s_weights = sem("s_weights")
        s_root_zero = sem("s_root_zero")
        s_const = sem("s_const")
        s_pool = sem("s_pool")
        s_node = sem("s_node")
        s_v = sem("s_v")
        s_basis = sem("s_basis")
        s_centred = sem("s_centred")
        s_squares = sem("s_squares")
        s_var = sem("s_var")
        s_std = sem("s_std")
        s_h = sem("s_h")
        s_table = sem("s_table")
        s_finished = sem("s_finished")
        s_hT = sem("s_hT")
        s_hT_sb = sem("s_hT_sb")
        s_root = sem("s_root")
        s_init = sem("s_init")
        s_acc_init = sem("s_acc_init")
        s_tab_min = sem("s_tab_min")
        s_tab_T = sem("s_tab_T")
        s_tab_ends = sem("s_tab_ends")
        s_tab_wide = sem("s_tab_wide")
        s_tab = sem("s_tab")
        s_index = sem("s_index")
        s_gathered = [[sem(f"s_gathered{a}_{c}") for c in range(CHUNKS)] for a in range(2)]
        s_rel = sem("s_rel")
        s_coef = sem("s_coef")
        s_vec_chunk = sem("s_vec_chunk")
        s_chunk_free = sem("s_chunk_free")
        s_A_sb = sem("s_A_sb")
        s_AT = sem("s_AT")
        s_AT_sb = sem("s_AT_sb")
        s_O = sem("s_O")
        s_sum = sem("s_sum")
        s_acc_load = sem("s_acc_load")
        s_acc_store = sem("s_acc_store")
        s_out = sem("s_out")

        block = ctx.enter_context(nc.Block())

        def node_view(dram, a, b):
            return dram[0:NODES_UP, :].rearrange("(p r) f -> p r f", r=ROWS)[:, a:b, :]

        def counter(eng, name):
            reg = eng.alloc_register(name)
            eng.reg_mov(reg, 0)
            return reg

        @block.sync
        def _(eng):
            eng.dma_start(dst_sb, dst).then_inc(s_edges[1], 16)
            for i, (a, b) in enumerate(PARTS):
                eng.dma_start(xres[:, a:b, :], node_view(x, a, b)).then_inc(s_x[i], 16)
                if i == 0:
                    eng.dma_start(attr_sb, attr).then_inc(s_edges[2], 16)
            eng.dma_start(etype_sb, etype).then_inc(s_edges[3], 16)
            eng.dma_start(srcs[:, 0:TILES], src).then_inc(s_edges[0], 16)
            eng.dma_start(srcs[:, TILES:], src[:, 0:2 * GROUP]).then_inc(s_edges[0], 16)
            eng.dma_start(acc_in[:, :], x[0:P, :]).then_inc(s_acc_load, 16)

            passes = counter(eng, "sync_passes")
            first_row = counter(eng, "sync_first_row")
            stores = counter(eng, "sync_stores")
            sums = counter(eng, "sync_sums")
            for l in range(LAYERS):
                if l in table:
                    for i, (a, b) in enumerate(PARTS):
                        eng.wait_ge(s_h, len(PARTS) * (l // 2) + i + 1)
                        eng.dma_start(node_view(table[l], a, b), h[:, a:b, :]).then_inc(s_table, 16)
                eng.wait_ge(s_init, BATCHES * (l + 1))
                eng.dma_start(node_view(acc[l], 0, ROWS), acc_init[:, :, :]).then_inc(s_acc_init, 16)
                eng.dma_start(acc[l][NODES_UP:ACC_ROWS, :], zeros[:, :]).then_inc(s_acc_store, 16)
                eng.wait_ge(s_acc_init, 16 * (l + 1))
                if l == 0:
                    eng.wait_ge(s_tab, 1)
                with eng.Fori(0, GROUPS) as g:
                    start = eng.value_load(tab[0:1, bass.ds(g, 1), 0:1].rearrange("p a b -> p (a b)"),
                                           min_val=0, max_val=NODES)
                    count = eng.value_load(tab[0:1, bass.ds(g, 1), 1:2].rearrange("p a b -> p (a b)"),
                                           min_val=1, max_val=MAX_PASSES)
                    eng.reg_mov(first_row, start)
                    with eng.Fori(0, count):
                        n = eng.snap(passes, min_val=0, max_val=LAST_N)
                        window = acc[l][bass.ds(eng.snap(first_row, min_val=0, max_val=NODES), WINDOW), :]
                        eng.reg_mov(stores, n * 16 + 16 * (l + 1))
                        eng.reg_mov(sums, n + (l + 2))
                        eng.wait_ge(s_acc_store, stores)
                        eng.wait_ge(s_sum, sums)
                        eng.dma_start(acc_in[:, :], window).then_inc(s_acc_load, 16)
                        eng.wait_ge(s_sum, n + (l + 3))
                        eng.dma_start(window, acc_sum[:, :]).then_inc(s_acc_store, 16)
                        eng.reg_add(passes, passes, 1)
                        eng.reg_add(first_row, first_row, WINDOW)
                n = eng.snap(passes, min_val=0, max_val=LAST_N)
                eng.reg_mov(stores, n * 16 + 16 * (l + 1))
                eng.wait_ge(s_acc_store, stores)
                eng.sem_inc(s_finished, 1)
                eng.wait_ge(s_table, 16 * len(PARTS) * (l // 2 + 1))
                eng.wait_ge(s_root, BATCHES * (l + 1))
                for i, (a, b) in enumerate(PARTS):
                    eng.dma_start(h[:, a:b, :], node_view(acc[l], a, b)).then_inc(s_acc_back[i], 16)
            for i, (a, b) in enumerate(PARTS):
                eng.wait_ge(s_h, 2 * len(PARTS) + i + 1)
                eng.dma_start(node_view(out, a, b), h[:, a:b, :]).then_inc(s_out, 16)
            eng.wait_ge(s_out, 16 * len(PARTS))

        @block.gpsimd
        def _(eng):
            eng.memset(ident[:, :], 0.0).then_inc(s_pool, 1)
            eng.wait_ge(s_pool, 1)
            eng.affine_select(out=ident[:, :], in_=ident[:, :], compare_op=ALU.not_equal, fill=1.0,
                              base=0, pattern=[[-1, P]], channel_multiplier=1).then_inc(s_const, 1)
            eng.iota(node_i[:, :], pattern=[[1, WINDOW]], base=0, channel_multiplier=0).then_inc(s_const, 1)
            b0, b1, b2 = (basis[:, :, :, i] for i in range(3))
            eng.wait_ge(s_edges[2], 16)
            eng.tensor_scalar(b0, attr_sb, 0.5, None, MUL).then_inc(s_pool, 1)
            eng.tensor_tensor(b1, attr_sb, attr_sb, MUL).then_inc(s_pool, 1)
            eng.wait_ge(s_pool, 3)
            eng.tensor_tensor(b2, b0, attr_sb, MUL).then_inc(s_pool, 1)
            eng.tensor_tensor(b1, attr_sb, b1, SUB).then_inc(s_pool, 1)
            eng.wait_ge(s_pool, 5)
            eng.tensor_tensor(b0, b2, attr_sb, SUB).then_inc(s_pool, 1)
            eng.tensor_scalar(b1, b1, 0.5, None, ADD).then_inc(s_basis, 1)
            eng.wait_ge(s_pool, 6)
            eng.tensor_scalar(b0, b0, 0.5, None, ADD).then_inc(s_basis, 1)
            eng.wait_ge(s_edges[3], 16)
            eng.tensor_copy(relation[:, :], etype_sb).then_inc(s_basis, 1)
            groups = counter(eng, "gpsimd_groups")
            for l in range(LAYERS):
                if l in table:
                    source = table[l]
                    eng.wait_ge(s_table, 16 * len(PARTS) * (l // 2 + 1))
                else:
                    source = acc[l - 1]
                    eng.wait_ge(s_finished, l)
                with eng.Fori(0, PAIRS):
                    for side in range(2):
                        group = eng.snap(groups, min_val=0, max_val=LAYERS * GROUPS)
                        eng.wait_ge(s_index, group + 1)
                        eng.reg_add(groups, groups, 1)
                        for t in range(GROUP):
                            eng.indirect_dma_start(
                                rows[:, side, t, :], None, source,
                                bass.IndirectOffsetOnAxis(ap=index[:, side, t:t + 1], axis=0),
                            ).then_inc(s_gathered[side][t // CHUNK], 16)

        @block.scalar
        def _(eng):
            eng.wait_ge(s_root_zero, 1)
            for l in range(LAYERS):
                full, rest = divmod(LAYER_K[l] * D, P)
                eng.dma_start(root_sb[l][0:D, 0:D], roots[l]).then_inc(s_weights, 16)
                eng.dma_start(root_sb[l][D:P, D:2 * D], roots[l]).then_inc(s_weights, 16)
                eng.dma_start(bias_sb[l][:, :], biases[l].rearrange("(a f) -> a f", a=1).to_broadcast([P, D]))\
                   .then_inc(s_weights, 16)
                eng.dma_start(W_sb[l][:, 0:full, :],
                              weights[l][0:full * P, :].rearrange("(c p) f -> p c f", p=P)).then_inc(s_weights, 16)
                if rest:
                    eng.dma_start(W_sb[l][0:rest, full, :], weights[l][full * P:, :]).then_inc(s_weights, 16)

            def norm(done):
                for i, (a, b) in enumerate(PARTS):
                    count = len(PARTS) * done + i
                    eng.wait_ge(s_centred, count + 1)
                    if count >= 2:
                        eng.wait_ge(s_var, count - 1)
                    eng.activation(squares[i % 2][:, 0:(b - a) * D], h[:, a:b, :].rearrange("p r f -> p (r f)"),
                                   ACT.Square).then_inc(s_squares, 1)
                    if i:
                        deviation(done, i - 1)
                deviation(done, len(PARTS) - 1)

            def deviation(done, i):
                a, b = PARTS[i]
                eng.wait_ge(s_var, len(PARTS) * done + i + 1)
                eng.activation(std[:, a:b], var[:, a:b], ACT.Sqrt, bias=eps[:, 0:1], scale=1.0 / D)                   .then_inc(s_std, 1)

            def evacuate_A(l, n):
                eng.wait_ge(s_chunk_free, n * CHUNKS + CHUNKS)
                eng.wait_ge(s_AT, n + (l + 1))
                banks, width = SPLITS[LAYER_K[l]], LAYER_K[l] * D
                eng.activation(A_sb[:, 0:width].rearrange("p (b n) -> p b n", b=banks),
                               A[:, bass.ds((n + 1) % 2, 1), 0:banks * BANK]
                               .rearrange("p a (b n) -> p (a b) n", b=banks)[:, :, 0:width // banks],
                               ACT.Copy).then_inc(s_A_sb, 1)

            def evacuate_AT(l, n):
                full, rest = divmod(LAYER_K[l] * D, P)
                eng.wait_ge(s_AT, n + (l + 2))
                eng.wait_ge(s_O, n + (l + 1))
                last = eng.activation(AT_sb[:, 0:full, :].rearrange("p c n -> p (c n)"),
                                      AT[:, 0, 0:full * P], ACT.Copy)
                if rest:
                    last = eng.activation(AT_sb[0:rest, full, :], AT[0:rest, 1, 0:P], ACT.Copy)
                last.then_inc(s_AT_sb, 1)

            eng.wait_ge(s_node, 1)
            eng.sem_inc(s_A_sb, 1)
            eng.sem_inc(s_AT_sb, 1)
            passes = counter(eng, "scalar_passes")
            for l in range(LAYERS):
                if l in table:
                    norm(l // 2)
                for b in range(BATCHES):
                    eng.wait_ge(s_hT, l * BATCHES + b + 1)
                    if b >= 2:
                        eng.wait_ge(s_root, l * BATCHES + b - 1)
                    w = min(BATCH, ROWS - b * BATCH) * D
                    eng.activation(hT_sb[:, b % 2, 0:w], AT[:, b % 2, 0:w], ACT.Relu).then_inc(s_hT_sb, 1)
                if l == 0:
                    eng.wait_ge(s_tab, 1)
                with eng.Fori(0, GROUPS) as g:
                    count = eng.value_load(tab[0:1, bass.ds(g, 1), 1:2].rearrange("p a b -> p (a b)"),
                                           min_val=1, max_val=MAX_PASSES)
                    with eng.Fori(0, count):
                        n = eng.snap(passes, min_val=0, max_val=LAST_N)
                        evacuate_A(l, n)
                        evacuate_AT(l, n)
                        eng.reg_add(passes, passes, 1)
                n = eng.snap(passes, min_val=0, max_val=LAST_N)
                evacuate_A(l, n)
                evacuate_AT(l, n)

        @block.tensor
        def _(eng):
            eng.wait_ge(s_const, 2)
            eng.wait_ge(s_node, 1)

            def transpose_batch(l, b):
                part = next(i for i, (lo, hi) in enumerate(PARTS) if b * BATCH < hi)
                if l in table:
                    eng.wait_ge(s_h, len(PARTS) * (l // 2) + part + 1)
                else:
                    eng.wait_ge(s_acc_back[part], 16 * l)
                if b >= 2:
                    eng.wait_ge(s_hT_sb, l * BATCHES + b - 1)
                n = min(BATCH, ROWS - b * BATCH) // 2
                for t in range(n):
                    r = b * BATCH + 2 * t
                    last = eng.transpose(AT[:, b % 2, t * P:(t + 1) * P],
                                         h[:, r:r + 2, :].rearrange("p r f -> p (r f)"), ident[:, :])
                last.then_inc(s_hT, 1)

            def root_batch(l, b):
                eng.wait_ge(s_hT_sb, l * BATCHES + b + 1)
                if b >= 2:
                    eng.wait_ge(s_init, l * BATCHES + b - 1)
                n = min(BATCH, ROWS - b * BATCH) // 2
                for t in range(n):
                    last = eng.matmul(O[:, b % 2, t * 2 * D:(t + 1) * 2 * D], hT_sb[:, b % 2, t * P:(t + 1) * P],
                                      root_sb[l][:, :], start=True, stop=True)
                last.then_inc(s_root, 1)

            def group_tables():
                eng.wait_ge(s_tab_min, 1)
                for i in range(2):
                    last = eng.transpose(AT[0:GROUPS, 0, i * P:(i + 1) * P], least[:, i, :], ident[:, :])
                last.then_inc(s_tab_T, 1)
                eng.wait_ge(s_tab_ends, 1)
                for i in range(2):
                    last = eng.matmul(O[:, 0, i * P:i * P + GROUPS], ends_wide[:, i, :], ident[0:GROUPS, 0:GROUPS],
                                      start=True, stop=True)
                last.then_inc(s_tab_wide, 1)

            def transpose_A(l, n):
                full, rest = divmod(LAYER_K[l] * D, P)
                eng.wait_ge(s_A_sb, n + (l + 2))
                eng.wait_ge(s_AT_sb, n + (l + 1))
                for c in range(full):
                    last = eng.transpose(AT[:, 0, c * P:(c + 1) * P], A_sb[:, c * P:(c + 1) * P], ident[:, :])
                if rest:
                    last = eng.transpose(AT[0:rest, 1, 0:P], A_sb[:, full * P:full * P + rest], ident[:, :])
                last.then_inc(s_AT, 1)

            def project(l, n):
                full, rest = divmod(LAYER_K[l] * D, P)
                eng.wait_ge(s_AT_sb, n + (l + 2))
                eng.wait_ge(s_sum, n + (l + 1))
                for c in range(full):
                    last = eng.matmul(O[:, 0, 0:D], AT_sb[:, c, :], W_sb[l][:, c, :],
                                      start=(c == 0), stop=(c == full - 1 and not rest))
                if rest:
                    last = eng.matmul(O[:, 0, 0:D], AT_sb[0:rest, full, :], W_sb[l][0:rest, full, :],
                                      start=False, stop=True)
                last.then_inc(s_O, 1)

            passes = counter(eng, "tensor_passes")
            for l in range(LAYERS):
                if l == 0:
                    group_tables()
                    eng.wait_ge(s_tab, 1)
                    eng.wait_ge(s_weights, 16 * sum(4 + (k * D % P > 0) for k in LAYER_K))
                    eng.sem_inc(s_chunk_free, CHUNKS)
                    eng.sem_inc(s_AT, 1)
                    eng.sem_inc(s_O, 1)
                transpose_batch(l, 0)
                for b in range(BATCHES):
                    if b + 1 < BATCHES:
                        transpose_batch(l, b + 1)
                    root_batch(l, b)
                banks, width = SPLITS[LAYER_K[l]], LAYER_K[l] * D // SPLITS[LAYER_K[l]]
                with eng.Fori(0, GROUPS) as g:
                    count = eng.value_load(tab[0:1, bass.ds(g, 1), 1:2].rearrange("p a b -> p (a b)"),
                                           min_val=1, max_val=MAX_PASSES)
                    with eng.Fori(0, count):
                        n = eng.snap(passes, min_val=0, max_val=LAST_N)
                        buf = eng.snap(n % 2, min_val=0, max_val=1)
                        eng.wait_ge(s_A_sb, n + (l + 1))
                        for c in range(CHUNKS):
                            eng.wait_ge(s_vec_chunk, n * CHUNKS + (c + 1))
                            for t in range(c * CHUNK, (c + 1) * CHUNK):
                                for i in range(banks):
                                    last = eng.matmul(A[:, bass.ds(buf, 1), i * BANK:i * BANK + width]
                                                      .rearrange("p a n -> p (a n)"),
                                                      S[:, t, :], M[:, t, i * width:(i + 1) * width],
                                                      start=(t == 0), stop=(t == GROUP - 1))
                            last.then_inc(s_chunk_free, 1)
                            if c == 1:
                                transpose_A(l, n)
                            if c == 3:
                                project(l, n)
                        eng.reg_add(passes, passes, 1)
                n = eng.snap(passes, min_val=0, max_val=LAST_N)
                transpose_A(l, n)
                project(l, n)

        @block.vector
        def _(eng):
            steps = [0]

            def step(ins):
                steps[0] += 1
                ins.then_inc(s_v, 1)

            def settled():
                eng.wait_ge(s_v, steps[0])

            for l in range(LAYERS):
                step(eng.memset(root_sb[l][:, :], 0.0))
            settled()
            eng.memset(eps[:, :], EPS).then_inc(s_root_zero, 1)
            eng.memset(zeros[:, :], 0.0)
            eng.memset(A[:, :, :], 0.0).then_inc(s_node, 1)
            eng.wait_ge(s_const, 2)
            step(eng.tensor_copy(node[:, :], node_i[:, :]))
            eng.sem_inc(s_sum, 1)
            eng.sem_inc(s_rel, 1)

            def wide(v, n):
                return v.unsqueeze(2).to_broadcast([P, v.shape[1], n])

            def norm(done):
                for i, (a, b) in enumerate(PARTS):
                    if not done:
                        eng.wait_ge(s_x[i], 16)
                    else:
                        eng.wait_ge(s_acc_back[i], 16 * 2)
                        step(eng.scalar_tensor_tensor(out=xres[:, a:b, :], in0=h[:, a:b, :], scalar=0.0,
                                                      in1=xres[:, a:b, :], op0=MAX, op1=ADD))
                    settled()
                    step(eng.tensor_reduce(mean[:, a:b], xres[:, a:b, :], AX.X, ADD))
                    settled()
                    step(eng.tensor_scalar(mean[:, a:b], mean[:, a:b], 1.0 / D, None, MUL))
                    settled()
                    eng.tensor_tensor(h[:, a:b, :], xres[:, a:b, :], wide(mean[:, a:b], D), SUB)\
                       .then_inc(s_centred, 1)
                    if i:
                        variance(done, i - 1)
                    if i > 1:
                        scaled(done, i - 2)
                variance(done, len(PARTS) - 1)
                scaled(done, len(PARTS) - 2)
                scaled(done, len(PARTS) - 1)

            def variance(done, i):
                a, b = PARTS[i]
                eng.wait_ge(s_squares, len(PARTS) * done + i + 1)
                eng.tensor_reduce(var[:, a:b], squares[i % 2][:, 0:(b - a) * D].rearrange("p (r f) -> p r f", f=D),
                                  AX.X, ADD).then_inc(s_var, 1)

            def scaled(done, i):
                a, b = PARTS[i]
                eng.wait_ge(s_std, len(PARTS) * done + i + 1)
                step(eng.reciprocal(std[:, a:b], std[:, a:b]))
                settled()
                eng.scalar_tensor_tensor(out=h[:, a:b, :], in0=h[:, a:b, :], scalar=0.0,
                                         in1=wide(std[:, a:b], D), op0=MAX, op1=MUL).then_inc(s_h, 1)

            def group_tables():
                eng.wait_ge(s_edges[1], 16)
                step(eng.tensor_copy(rel[:, :], dst_sb))
                settled()
                by_group = rel[:, :].rearrange("p (g t) -> p g t", t=GROUP)
                step(eng.tensor_reduce(least[:, 0, :], by_group, AX.X, ALU.min))
                eng.tensor_reduce(least[:, 1, :], by_group, AX.X, MAX).then_inc(s_tab_min, 1)
                eng.wait_ge(s_tab_T, 1)
                step(eng.tensor_reduce(ends[:, 0:1], AT[0:GROUPS, 0, 0:P], AX.X, ALU.min))
                step(eng.tensor_reduce(ends[:, 1:2], AT[0:GROUPS, 0, P:2 * P], AX.X, MAX))
                settled()
                eng.tensor_copy(ends_wide[:, :, :], ends[:, :].unsqueeze(2).to_broadcast([GROUPS, 2, P]))\
                   .then_inc(s_tab_ends, 1)
                eng.wait_ge(s_tab_wide, 1)
                step(eng.tensor_tensor(by_group, by_group,
                                       O[:, 0, 0:GROUPS].unsqueeze(2).to_broadcast([P, GROUPS, GROUP]), SUB))
                step(eng.tensor_copy(ends_i[0:1, :, :],
                                     O[0:1, 0, 0:2 * P].rearrange("p (a g) -> p a g", a=2)[:, :, 0:GROUPS]))
                settled()
                step(eng.tensor_tensor(ends_i[0:1, 1, :], ends_i[0:1, 1, :], ends_i[0:1, 0, :], SUB))
                step(eng.tensor_copy(tab[0:1, :, 0], ends_i[0:1, 0, :]))
                settled()
                step(eng.tensor_scalar(ends_i[0:1, 1, :], ends_i[0:1, 1, :], WINDOW.bit_length() - 1, None,
                                       ALU.arith_shift_right))
                settled()
                step(eng.tensor_scalar(span[0:1, :], ends_i[0:1, 1, :], 1.0, None, ADD))
                settled()
                eng.tensor_copy(tab[0:1, :, 1], span[0:1, :]).then_inc(s_tab, 1)

            def group_coef(l, tile0):
                if LAYER_K[l] == SPLINE_K:
                    return eng.tensor_tensor(
                        coef[:, :, :].rearrange("p t (i j) -> p t i j", j=3),
                        basis[:, 0, bass.ds(tile0, GROUP), :].unsqueeze(3).to_broadcast([P, GROUP, 3, 3]),
                        basis[:, 1, bass.ds(tile0, GROUP), :].unsqueeze(2).to_broadcast([P, GROUP, 3, 3]), MUL)
                return eng.tensor_tensor(
                    coef[:, :, 0:RELATIONS],
                    relation[:, bass.ds(tile0, GROUP)].unsqueeze(2).to_broadcast([P, GROUP, RELATIONS]),
                    node[:, 0:RELATIONS].unsqueeze(1).to_broadcast([P, GROUP, RELATIONS]), ALU.is_equal)

            def flush(l, n):
                eng.wait_ge(s_O, n + (l + 2))
                eng.wait_ge(s_acc_load, n * 16 + 16)
                eng.tensor_tensor(acc_sum[:, :], O[:, 0, 0:D], acc_in[:, :], ADD).then_inc(s_sum, 1)

            passes = counter(eng, "vector_passes")
            for l in range(LAYERS):
                if l == 0:
                    group_tables()
                    norm(0)
                    eng.wait_ge(s_edges[0], 32)
                    for side in range(2):
                        eng.tensor_copy(index[:, side, :], srcs[:, side * GROUP:(side + 1) * GROUP])\
                           .then_inc(s_index, 1)
                    eng.wait_ge(s_weights, 16 * sum(4 + (k * D % P > 0) for k in LAYER_K))
                if l == 2:
                    norm(1)
                if l:
                    eng.wait_ge(s_acc_init, 16 * l)
                for b in range(BATCHES):
                    eng.wait_ge(s_root, l * BATCHES + b + 1)
                    r0, r1 = b * BATCH, min(ROWS, (b + 1) * BATCH)
                    eng.tensor_tensor(acc_init[:, r0:r1, :],
                                      O[:, b % 2, 0:(r1 - r0) * D].rearrange("p (r f) -> p r f", f=D),
                                      bias_sb[l][:, :].unsqueeze(1).to_broadcast([P, r1 - r0, D]), ADD)\
                       .then_inc(s_init, 1)
                if l == 0:
                    eng.wait_ge(s_basis, 3)
                ks = LAYER_K[l]
                with eng.Fori(0, PAIRS) as pair:
                    for side in range(2):
                        g = eng.snap(pair * 2 + side, min_val=0, max_val=GROUPS - 1)
                        count = eng.value_load(tab[0:1, bass.ds(g, 1), 1:2].rearrange("p a b -> p (a b)"),
                                               min_val=1, max_val=MAX_PASSES)
                        tile0 = eng.snap(g * GROUP, min_val=0, max_val=TILES - GROUP)
                        n = eng.snap(passes, min_val=0, max_val=LAST_N)
                        eng.wait_ge(s_rel, n + g + (l * GROUPS + 1))
                        eng.tensor_copy(relq[:, :], rel[:, bass.ds(tile0, GROUP)]).then_inc(s_rel, 1)
                        group_coef(l, tile0).then_inc(s_coef, 1)
                        with eng.Fori(0, count):
                            n = eng.snap(passes, min_val=0, max_val=LAST_N)
                            eng.wait_ge(s_rel, n + g + (l * GROUPS + 2))
                            eng.wait_ge(s_coef, g + (l * GROUPS + 1))
                            for c in range(CHUNKS):
                                t0, t1 = c * CHUNK, (c + 1) * CHUNK
                                eng.wait_ge(s_chunk_free, n * CHUNKS + (c + 1))
                                eng.tensor_tensor(S[:, t0:t1, :],
                                                  node[:, :].unsqueeze(1).to_broadcast([P, CHUNK, WINDOW]),
                                                  relq[:, t0:t1].unsqueeze(2).to_broadcast([P, CHUNK, WINDOW]),
                                                  ALU.is_equal)
                                eng.wait_ge(s_gathered[side][c], pair * (16 * CHUNK) + 16 * CHUNK * (l * PAIRS + 1))
                                for t in range(t0, t1):
                                    last = eng.scalar_tensor_tensor(
                                        out=M[:, t, 0:ks * D].rearrange("p (k f) -> p k f", f=D),
                                        in0=rows[:, side, t:t + 1, :].to_broadcast([P, ks, D]), scalar=0.0,
                                        in1=coef[:, t, 0:ks].unsqueeze(2).to_broadcast([P, ks, D]),
                                        op0=MAX, op1=MUL)
                                last.then_inc(s_vec_chunk, 1)
                            flush(l, n)
                            eng.wait_ge(s_vec_chunk, n * CHUNKS + CHUNKS)
                            eng.tensor_scalar(relq[:, :], relq[:, :], float(WINDOW), None, SUB).then_inc(s_rel, 1)
                            eng.reg_add(passes, passes, 1)
                        n = eng.snap(passes, min_val=0, max_val=LAST_N)
                        eng.wait_ge(s_vec_chunk, n * CHUNKS)
                        eng.tensor_copy(index[:, side, :], srcs[:, bass.ds(tile0 + 2 * GROUP, GROUP)])\
                           .then_inc(s_index, 1)
                n = eng.snap(passes, min_val=0, max_val=LAST_N)
                flush(l, n)
            for i, (a, b) in enumerate(PARTS):
                eng.wait_ge(s_acc_back[i], 16 * LAYERS)
                eng.tensor_tensor(h[:, a:b, :], xres[:, a:b, :], h[:, a:b, :], ADD).then_inc(s_h, 1)
    return nc


def kernel(**inputs):
    import numpy as np
    import concourse.bacc as bacc
    from concourse.bass_utils import run_bass_kernel_spmd

    def by_tile(a, fill):
        a = np.asarray(a)
        up = np.full((TILES * P,) + a.shape[1:], fill, a.dtype)
        up[:EDGES] = a
        up = up.reshape((GROUPS, P, GROUP) + a.shape[1:])
        return np.ascontiguousarray(np.moveaxis(up, 1, 0)).reshape((P, TILES) + a.shape[1:])

    x = np.zeros((NODES_UP, D), np.asarray(inputs["x"]).dtype)
    x[:NODES] = inputs["x"]
    arrays = {
        "x": x,
        "src": by_tile(inputs["src"], 0),
        "dst": by_tile(inputs["dst"], NODES),
        "attr": np.ascontiguousarray(np.moveaxis(by_tile(inputs["edge_attr_2"], 0), 2, 1)),
        "etype": by_tile(inputs["edge_type_8"], 0),
    }
    for part in ("L0", "L1"):
        for n in ("1", "2"):
            w = np.asarray(inputs[f"{part}_gnn_W{n}"])
            arrays[f"W_{part}_{n}"] = np.ascontiguousarray(w.reshape(-1, D))
            arrays[f"root_{part}_{n}"] = np.ascontiguousarray(inputs[f"{part}_gnn_root{n}"])
            arrays[f"b_{part}_{n}"] = np.ascontiguousarray(inputs[f"{part}_gnn_b{n}"])

    nc = bacc.Bacc("TRN2", target_bir_lowering=False, num_devices=1)
    aps = {name: nc.dram_tensor(name, a.shape, mybir.dt.from_np(a.dtype), kind="ExternalInput").ap()
           for name, a in arrays.items()}
    out = nc.dram_tensor("out", (NODES_UP, D), FP32, kind="ExternalOutput").ap()
    layers = [f"{part}_{n}" for part in ("L0", "L1") for n in ("1", "2")]
    gnn_kernel(nc, aps["x"], aps["src"], aps["dst"], aps["attr"], aps["etype"],
               [aps["W_" + s] for s in layers], [aps["root_" + s] for s in layers],
               [aps["b_" + s] for s in layers], out)
    got = run_bass_kernel_spmd(nc, [arrays], core_ids=[0])
    return got.results[0]["out"][:NODES]
```

```python
from contextlib import ExitStack

import concourse.bass as bass
from concourse import mybir

FP32 = mybir.dt.float32
INT32 = mybir.dt.int32
ALU = mybir.AluOpType
ACT = mybir.ActivationFunctionType
AX = mybir.AxisListType

NODES, EDGES, D = 12500, 200000, 64
P = 128
WINDOW = 128
ROWS = -(-NODES // P)
NODES_UP = ROWS * P
GROUP = 14
CHUNK = 2
CHUNKS = GROUP // CHUNK
GROUPS = -(-EDGES // (P * GROUP))
RING = 3
TRIPS = (GROUPS - 1) // RING
TAIL = -(-EDGES // P) - (GROUPS - 1) * GROUP
TILES = GROUPS * GROUP
ACC_ROWS = NODES_UP + WINDOW
SPLINE_K, RELATIONS = 9, 8
LAYER_K = [SPLINE_K, SPLINE_K, RELATIONS, RELATIONS]
LAYERS = len(LAYER_K)
LAST_N = 1 << 17
MAX_PASSES = -(-(NODES + 1) // WINDOW)
PARTS = [(0, 24), (24, 48), (48, 72), (72, ROWS)]
LONGEST = max(b - a for a, b in PARTS)
BATCH = 8
BATCHES = -(-ROWS // BATCH)
EPS = 1e-5
MUL, ADD, SUB, MAX = ALU.mult, ALU.add, ALU.subtract, ALU.max
BANK = 512
SPLITS = {SPLINE_K: 2, RELATIONS: 1}
assert (GROUPS - 1) % RING == 0 and GROUP % CHUNK == 0


def gnn_kernel(nc, x, src, dst, attr, etype, weights, roots, biases, out):
    ctx = ExitStack()
    with ctx:
        def sb(name, shape, dt=FP32):
            return ctx.enter_context(nc.sbuf_tensor(name, shape, dt))

        def sem(name):
            return ctx.enter_context(nc.semaphore(name))

        table = {l: nc.dram_tensor(f"table{l}", (NODES_UP, D), FP32, kind="Internal").ap() for l in (0, 2)}
        acc = [nc.dram_tensor(f"acc{l}", (ACC_ROWS, D), FP32, kind="Internal").ap() for l in range(LAYERS - 1)]
        acc.append(out)

        xres = sb("xres", [P, ROWS, D])
        h = sb("h", [P, ROWS, D])
        basis = sb("basis", [P, 2, TILES, 3])
        rel = sb("rel", [P, TILES])
        srcs = sb("srcs", [P, TILES + RING * GROUP], INT32)
        relation = sb("relation", [P, TILES])
        rows = sb("rows", [P, RING, GROUP, D])
        index = sb("index", [P, RING, GROUP], INT32)
        coef = sb("coef", [P, GROUP, SPLINE_K])
        relq = sb("relq", [P, GROUP])
        S = sb("S", [P, GROUP, WINDOW])
        M = sb("M", [P, GROUP, SPLINE_K * D])
        A_sb = sb("A_sb", [P, SPLINE_K * D])
        AT_sb = sb("AT_sb", [P, 5, P])
        acc_in = sb("acc_in", [P, D])
        acc_sum = sb("acc_sum", [P, D])
        acc_init = sb("acc_init", [P, ROWS, D])
        flat = M[:, :, :].rearrange("p t n -> p (t n)")
        attr_sb = flat[:, 0:2 * TILES].rearrange("p (a t) -> p a t", a=2)
        etype_sb = flat[:, 2 * TILES:3 * TILES].bitcast(INT32)
        squares = [flat[:, 3 * TILES + i * LONGEST * D:3 * TILES + (i + 1) * LONGEST * D] for i in range(2)]
        dst_sb = acc_init[:, :, :].rearrange("p r f -> p (r f)")[:, 0:TILES].bitcast(INT32)
        hT_sb = sb("hT_sb", [P, 2, 4 * P])
        W_sb = [sb(f"W{l}", [P, 5, D]) for l in range(LAYERS)]
        root_sb = [sb(f"root{l}", [P, 2 * D]) for l in range(LAYERS)]
        bias_sb = [sb(f"bias{l}", [P, D]) for l in range(LAYERS)]
        ident = sb("ident", [P, P])
        node_i = sb("node_i", [P, WINDOW], INT32)
        node = sb("node", [P, WINDOW])
        eps = sb("eps", [P, 1])
        less_one = sb("less_one", [P, 1])
        less_half = sb("less_half", [P, 1])
        zeros = sb("zeros", [P, D])
        least = sb("least", [P, 2, GROUPS])
        ends = sb("ends", [GROUPS, 2])
        ends_wide = sb("ends_wide", [GROUPS, 2, P])
        ends_i = sb("ends_i", [1, 2, GROUPS], INT32)
        starts = sb("starts", [P, GROUPS])
        span = sb("span", [1, GROUPS])
        tab = sb("tab", [1, GROUPS, 2], INT32)
        mean = sb("mean", [P, ROWS])
        var = sb("var", [P, ROWS])
        std = sb("std", [P, ROWS])

        A = ctx.enter_context(nc.psum_tensor("A", [P, 2, 1024], FP32))
        AT = ctx.enter_context(nc.psum_tensor("AT", [P, 2, 512], FP32))
        O = ctx.enter_context(nc.psum_tensor("O", [P, 2, 512], FP32))

        s_x = [sem(f"s_x{i}") for i in range(len(PARTS))]
        s_acc_back = [sem(f"s_acc_back{i}") for i in range(len(PARTS))]
        s_edges = [sem(f"s_edges_{n}") for n in ("src", "dst", "attr", "type")]
        s_weights = sem("s_weights")
        s_root_zero = sem("s_root_zero")
        s_const = sem("s_const")
        s_pool = sem("s_pool")
        s_node = sem("s_node")
        s_v = sem("s_v")
        s_basis_square = sem("s_basis_square")
        s_target = sem("s_target")
        s_starts = sem("s_starts")
        s_basis = sem("s_basis")
        s_mean = sem("s_mean")
        s_centred = sem("s_centred")
        s_squares = sem("s_squares")
        s_var = sem("s_var")
        s_std = sem("s_std")
        s_h = sem("s_h")
        s_table = sem("s_table")
        s_finished = sem("s_finished")
        s_hT = sem("s_hT")
        s_hT_sb = sem("s_hT_sb")
        s_root = sem("s_root")
        s_init = sem("s_init")
        s_init_bias = sem("s_init_bias")
        s_acc_init = sem("s_acc_init")
        s_tab_min = sem("s_tab_min")
        s_tab_T = sem("s_tab_T")
        s_tab_ends = sem("s_tab_ends")
        s_tab_wide = sem("s_tab_wide")
        s_tab = sem("s_tab")
        s_index = sem("s_index")
        s_gathered = [[sem(f"s_gathered{a}_{c}") for c in range(CHUNKS)] for a in range(RING)]
        s_rel = sem("s_rel")
        s_coef = sem("s_coef")
        s_vec_chunk = sem("s_vec_chunk")
        s_chunk_free = sem("s_chunk_free")
        s_A_sb = sem("s_A_sb")
        s_AT = sem("s_AT")
        s_AT_sb = sem("s_AT_sb")
        s_O = sem("s_O")
        s_sum = sem("s_sum")
        s_acc_load = sem("s_acc_load")
        s_acc_store = sem("s_acc_store")

        block = ctx.enter_context(nc.Block())

        def node_view(dram, a, b):
            return dram[0:NODES_UP, :].rearrange("(p r) f -> p r f", r=ROWS)[:, a:b, :]

        def wide(v, n):
            return v.unsqueeze(2).to_broadcast([P, v.shape[1], n])

        def tiles_of(c, last):
            return range(c * CHUNK, min((c + 1) * CHUNK, TAIL if last else GROUP))

        def chunks_of(last):
            return -(-TAIL // CHUNK) if last else CHUNKS

        def chunk_steps(c, last):
            return CHUNKS - c if c == chunks_of(last) - 1 else 1

        def gathered(l, place, c, trip, last=False):
            per_layer = TRIPS * CHUNK + (len(tiles_of(c, True)) if place == 0 else 0)
            return trip * (16 * CHUNK) + 16 * (l * per_layer + len(tiles_of(c, last)))

        def counter(eng, name):
            reg = eng.alloc_register(name)
            eng.reg_mov(reg, 0)
            return reg

        @block.sync
        def _(eng):
            eng.dma_start(dst_sb, dst).then_inc(s_edges[1], 16)
            for i, (a, b) in enumerate(PARTS):
                eng.dma_start(xres[:, a:b, :], node_view(x, a, b)).then_inc(s_x[i], 16)
                if i == 0:
                    eng.dma_start(attr_sb, attr).then_inc(s_edges[2], 16)
            eng.dma_start(etype_sb, etype).then_inc(s_edges[3], 16)
            eng.dma_start(srcs[:, 0:TILES], src).then_inc(s_edges[0], 16)
            eng.dma_start(srcs[:, TILES:TILES + (RING - 1) * GROUP], src[:, GROUP:RING * GROUP])\
               .then_inc(s_edges[0], 16)
            eng.dma_start(srcs[:, TILES + (RING - 1) * GROUP:], src[:, 0:GROUP]).then_inc(s_edges[0], 16)
            eng.wait_ge(s_root_zero, 1)
            for l in range(LAYERS):
                full, rest = divmod(LAYER_K[l] * D, P)
                eng.dma_start(root_sb[l][0:D, 0:D], roots[l]).then_inc(s_weights, 16)
                eng.dma_start(root_sb[l][D:P, D:2 * D], roots[l]).then_inc(s_weights, 16)
                eng.dma_start(bias_sb[l][:, :], biases[l].rearrange("(a f) -> a f", a=1).to_broadcast([P, D]))\
                   .then_inc(s_weights, 16)
                eng.dma_start(W_sb[l][:, 0:full, :],
                              weights[l][0:full * P, :].rearrange("(c p) f -> p c f", p=P)).then_inc(s_weights, 16)
                if rest:
                    eng.dma_start(W_sb[l][0:rest, full, :], weights[l][full * P:, :]).then_inc(s_weights, 16)
            eng.dma_start(acc_in[:, :], x[0:P, :]).then_inc(s_acc_load, 16)

            passes = counter(eng, "sync_passes")
            first_row = counter(eng, "sync_first_row")
            stores = counter(eng, "sync_stores")
            sums = counter(eng, "sync_sums")
            for l in range(LAYERS):
                if l in table:
                    for i, (a, b) in enumerate(PARTS):
                        eng.wait_ge(s_h, len(PARTS) * (l // 2) + i + 1)
                        eng.dma_start(node_view(table[l], a, b), h[:, a:b, :]).then_inc(s_table, 16)
                eng.wait_ge(s_init, BATCHES * (l + 1))
                eng.dma_start(node_view(acc[l], 0, ROWS), acc_init[:, :, :]).then_inc(s_acc_init, 16)
                eng.dma_start(acc[l][NODES_UP:ACC_ROWS, :], zeros[:, :]).then_inc(s_acc_store, 16)
                eng.wait_ge(s_acc_init, 16 * (l + 1))
                if l == 0:
                    eng.wait_ge(s_tab, 1)
                with eng.Fori(0, GROUPS) as g:
                    start = eng.value_load(tab[0:1, bass.ds(g, 1), 0:1].rearrange("p a b -> p (a b)"),
                                           min_val=0, max_val=NODES)
                    count = eng.value_load(tab[0:1, bass.ds(g, 1), 1:2].rearrange("p a b -> p (a b)"),
                                           min_val=1, max_val=MAX_PASSES)
                    eng.reg_mov(first_row, start)
                    with eng.Fori(0, count):
                        n = eng.snap(passes, min_val=0, max_val=LAST_N)
                        window = acc[l][bass.ds(eng.snap(first_row, min_val=0, max_val=NODES), WINDOW), :]
                        eng.reg_mov(stores, n * 16 + 16 * (l + 1))
                        eng.reg_mov(sums, n + (l + 2))
                        eng.wait_ge(s_acc_store, stores)
                        eng.wait_ge(s_sum, sums)
                        eng.dma_start(acc_in[:, :], window).then_inc(s_acc_load, 16)
                        eng.wait_ge(s_sum, n + (l + 3))
                        eng.dma_start(window, acc_sum[:, :]).then_inc(s_acc_store, 16)
                        eng.reg_add(passes, passes, 1)
                        eng.reg_add(first_row, first_row, WINDOW)
                n = eng.snap(passes, min_val=0, max_val=LAST_N)
                eng.reg_mov(stores, n * 16 + 16 * (l + 1))
                eng.wait_ge(s_acc_store, stores)
                eng.sem_inc(s_finished, 1)
                if l == LAYERS - 1:
                    break
                eng.wait_ge(s_table, 16 * len(PARTS) * (l // 2 + 1))
                eng.wait_ge(s_root, BATCHES * (l + 1))
                for i, (a, b) in enumerate(PARTS):
                    eng.dma_start(h[:, a:b, :], node_view(acc[l], a, b)).then_inc(s_acc_back[i], 16)

        @block.gpsimd
        def _(eng):
            eng.memset(ident[:, :], 0.0).then_inc(s_pool, 1)
            eng.wait_ge(s_pool, 1)
            eng.affine_select(out=ident[:, :], in_=ident[:, :], compare_op=ALU.not_equal, fill=1.0,
                              base=0, pattern=[[-1, P]], channel_multiplier=1).then_inc(s_const, 1)
            eng.iota(node_i[:, :], pattern=[[1, WINDOW]], base=0, channel_multiplier=0).then_inc(s_const, 1)
            groups = counter(eng, "gpsimd_groups")
            for l in range(LAYERS):
                if l in table:
                    for i, (a, b) in enumerate(PARTS):
                        eng.wait_ge(s_mean, len(PARTS) * (l // 2) + i + 1)
                        eng.tensor_tensor(h[:, a:b, :], xres[:, a:b, :], wide(mean[:, a:b], D), SUB)\
                           .then_inc(s_centred, 1)
                if l == 0:
                    by_group = rel[:, :].rearrange("p (g t) -> p g t", t=GROUP)
                    eng.wait_ge(s_tab_min, 2)
                    eng.wait_ge(s_starts, 1)
                    eng.tensor_tensor(by_group, by_group, wide(starts[:, :], GROUP), SUB).then_inc(s_rel, 1)
                if l in table:
                    source = table[l]
                    eng.wait_ge(s_table, 16 * len(PARTS) * (l // 2 + 1))
                else:
                    source = acc[l - 1]
                    eng.wait_ge(s_finished, l)

                def gather(place, last=False):
                    for c in range(chunks_of(last)):
                        for t in tiles_of(c, last):
                            eng.indirect_dma_start(
                                rows[:, place, t, :], None, source,
                                bass.IndirectOffsetOnAxis(ap=index[:, place, t:t + 1], axis=0),
                            ).then_inc(s_gathered[place][c], 16)

                eng.wait_ge(s_index, l * GROUPS + RING)
                with eng.Fori(0, TRIPS):
                    for place in range(RING):
                        group = eng.snap(groups, min_val=0, max_val=LAYERS * GROUPS)
                        eng.wait_ge(s_index, group + 1)
                        eng.reg_add(groups, groups, 1)
                        gather(place)
                eng.wait_ge(s_index, (l + 1) * GROUPS)
                gather(0, last=True)
                eng.reg_add(groups, groups, 1)

        @block.scalar
        def _(eng):
            def norm(done):
                for i, (a, b) in enumerate(PARTS):
                    count = len(PARTS) * done + i
                    if count == 1:
                        eng.wait_ge(s_edges[2], 16)
                        eng.activation(basis[:, :, :, 0], attr_sb, ACT.Square, bias=less_one[:, 0:1])\
                           .then_inc(s_basis_square, 1)
                        eng.activation(basis[:, :, :, 1], attr_sb, ACT.Square, bias=less_half[:, 0:1])\
                           .then_inc(s_basis_square, 1)
                    if count == 2:
                        eng.activation(basis[:, :, :, 2], attr_sb, ACT.Square).then_inc(s_basis_square, 1)
                    if count == 3:
                        eng.wait_ge(s_basis_square, 3)
                        eng.activation(basis[:, :, :, 1], basis[:, :, :, 1], ACT.Copy, bias=0.75, scale=-1.0)\
                           .then_inc(s_basis, 1)
                        eng.activation(basis[:, :, :, 0], basis[:, :, :, 0], ACT.Copy, scale=0.5).then_inc(s_basis, 1)
                        eng.wait_ge(s_tab_wide, 1)
                        eng.activation(starts[:, :], A[:, 0, BANK:BANK + GROUPS], ACT.Copy).then_inc(s_starts, 1)
                    eng.wait_ge(s_centred, count + 1)
                    if count >= 2:
                        eng.wait_ge(s_var, count - 1)
                    eng.activation(squares[i % 2][:, 0:(b - a) * D], h[:, a:b, :].rearrange("p r f -> p (r f)"),
                                   ACT.Square).then_inc(s_squares, 1)
                    if i:
                        deviation(done, i - 1)
                for b in range(2):
                    evacuate_hT(2 * done, b)
                deviation(done, len(PARTS) - 1)
                if not done:
                    eng.activation(basis[:, :, :, 2], basis[:, :, :, 2], ACT.Copy, scale=0.5).then_inc(s_basis, 1)

            def evacuate_hT(l, b):
                eng.wait_ge(s_hT, l * BATCHES + b + 1)
                if b >= 2:
                    eng.wait_ge(s_root, l * BATCHES + b - 1)
                w = min(BATCH, ROWS - b * BATCH) * D
                eng.activation(hT_sb[:, b % 2, 0:w], AT[:, b % 2, 0:w], ACT.Relu).then_inc(s_hT_sb, 1)

            def deviation(done, i):
                a, b = PARTS[i]
                eng.wait_ge(s_var, len(PARTS) * done + i + 1)
                eng.activation(std[:, a:b], var[:, a:b], ACT.Sqrt, bias=eps[:, 0:1], scale=1.0 / D)\
                   .then_inc(s_std, 1)

            def evacuate_A(l, n):
                eng.wait_ge(s_chunk_free, n * CHUNKS + CHUNKS)
                eng.wait_ge(s_AT, n + (l + 1))
                banks, width = SPLITS[LAYER_K[l]], LAYER_K[l] * D
                eng.activation(A_sb[:, 0:width].rearrange("p (b n) -> p b n", b=banks),
                               A[:, bass.ds((n + 1) % 2, 1), 0:banks * BANK]
                               .rearrange("p a (b n) -> p (a b) n", b=banks)[:, :, 0:width // banks],
                               ACT.Copy).then_inc(s_A_sb, 1)

            def evacuate_AT(l, n):
                full, rest = divmod(LAYER_K[l] * D, P)
                eng.wait_ge(s_AT, n + (l + 2))
                eng.wait_ge(s_O, n + (l + 1))
                last = eng.activation(AT_sb[:, 0:full, :].rearrange("p c n -> p (c n)"),
                                      AT[:, 0, 0:full * P], ACT.Copy)
                if rest:
                    last = eng.activation(AT_sb[0:rest, full, :], AT[0:rest, 1, 0:P], ACT.Copy)
                last.then_inc(s_AT_sb, 1)

            eng.wait_ge(s_node, 1)
            eng.sem_inc(s_A_sb, 1)
            eng.sem_inc(s_AT_sb, 1)
            eng.wait_ge(s_edges[1], 16)
            eng.activation(rel[:, :], dst_sb, ACT.Copy).then_inc(s_target, 1)
            passes = counter(eng, "scalar_passes")
            for l in range(LAYERS):
                if l in table:
                    norm(l // 2)
                for b in range(2 if l in table else 0, BATCHES):
                    evacuate_hT(l, b)
                if l == 0:
                    eng.wait_ge(s_edges[3], 16)
                    eng.activation(relation[:, :], etype_sb, ACT.Copy).then_inc(s_basis, 1)
                    eng.wait_ge(s_tab, 1)
                with eng.Fori(0, GROUPS) as g:
                    count = eng.value_load(tab[0:1, bass.ds(g, 1), 1:2].rearrange("p a b -> p (a b)"),
                                           min_val=1, max_val=MAX_PASSES)
                    with eng.Fori(0, count):
                        n = eng.snap(passes, min_val=0, max_val=LAST_N)
                        evacuate_A(l, n)
                        evacuate_AT(l, n)
                        eng.reg_add(passes, passes, 1)
                n = eng.snap(passes, min_val=0, max_val=LAST_N)
                evacuate_A(l, n)
                evacuate_AT(l, n)

        @block.tensor
        def _(eng):
            eng.wait_ge(s_const, 2)
            eng.wait_ge(s_node, 1)

            def transpose_batch(l, b):
                part = next(i for i, (lo, hi) in enumerate(PARTS) if b * BATCH < hi)
                if l in table:
                    eng.wait_ge(s_h, len(PARTS) * (l // 2) + part + 1)
                else:
                    eng.wait_ge(s_acc_back[part], 16 * l)
                if b >= 2:
                    eng.wait_ge(s_hT_sb, l * BATCHES + b - 1)
                n = min(BATCH, ROWS - b * BATCH) // 2
                for t in range(n):
                    r = b * BATCH + 2 * t
                    last = eng.transpose(AT[:, b % 2, t * P:(t + 1) * P],
                                         h[:, r:r + 2, :].rearrange("p r f -> p (r f)"), ident[:, :])
                last.then_inc(s_hT, 1)

            def root_batch(l, b):
                eng.wait_ge(s_hT_sb, l * BATCHES + b + 1)
                if b >= 2:
                    eng.wait_ge(s_init, l * BATCHES + b - 1)
                n = min(BATCH, ROWS - b * BATCH) // 2
                for t in range(n):
                    last = eng.matmul(O[:, b % 2, t * 2 * D:(t + 1) * 2 * D], hT_sb[:, b % 2, t * P:(t + 1) * P],
                                      root_sb[l][:, :], start=True, stop=True)
                last.then_inc(s_root, 1)

            def group_tables():
                eng.wait_ge(s_tab_min, 2)
                for i in range(2):
                    last = eng.transpose(A[0:GROUPS, 0, i * P:(i + 1) * P], least[:, i, :], ident[:, :])
                last.then_inc(s_tab_T, 1)
                eng.wait_ge(s_tab_ends, 1)
                for i in range(2):
                    last = eng.matmul(A[:, 0, BANK + i * P:BANK + i * P + GROUPS], ends_wide[:, i, :],
                                      ident[0:GROUPS, 0:GROUPS], start=True, stop=True)
                last.then_inc(s_tab_wide, 1)

            def transpose_A(l, n):
                full, rest = divmod(LAYER_K[l] * D, P)
                eng.wait_ge(s_A_sb, n + (l + 2))
                eng.wait_ge(s_AT_sb, n + (l + 1))
                for c in range(full):
                    last = eng.transpose(AT[:, 0, c * P:(c + 1) * P], A_sb[:, c * P:(c + 1) * P], ident[:, :])
                if rest:
                    last = eng.transpose(AT[0:rest, 1, 0:P], A_sb[:, full * P:full * P + rest], ident[:, :])
                last.then_inc(s_AT, 1)

            def project(l, n):
                full, rest = divmod(LAYER_K[l] * D, P)
                eng.wait_ge(s_AT_sb, n + (l + 2))
                eng.wait_ge(s_sum, n + (l + 1))
                for c in range(full):
                    last = eng.matmul(O[:, 0, 0:D], AT_sb[:, c, :], W_sb[l][:, c, :],
                                      start=(c == 0), stop=(c == full - 1 and not rest))
                if rest:
                    last = eng.matmul(O[:, 0, 0:D], AT_sb[0:rest, full, :], W_sb[l][0:rest, full, :],
                                      start=False, stop=True)
                last.then_inc(s_O, 1)

            passes = counter(eng, "tensor_passes")
            for l in range(LAYERS):
                if l == 0:
                    group_tables()
                    eng.wait_ge(s_weights, 16 * sum(4 + (k * D % P > 0) for k in LAYER_K))
                    eng.sem_inc(s_chunk_free, CHUNKS)
                    eng.sem_inc(s_AT, 1)
                    eng.sem_inc(s_O, 1)
                transpose_batch(l, 0)
                for b in range(BATCHES):
                    if b + 1 < BATCHES:
                        transpose_batch(l, b + 1)
                    root_batch(l, b)
                if l == 0:
                    eng.wait_ge(s_tab, 1)
                banks, width = SPLITS[LAYER_K[l]], LAYER_K[l] * D // SPLITS[LAYER_K[l]]

                def group(g, last=False):
                    count = eng.value_load(tab[0:1, bass.ds(g, 1), 1:2].rearrange("p a b -> p (a b)"),
                                           min_val=1, max_val=MAX_PASSES)
                    with eng.Fori(0, count):
                        n = eng.snap(passes, min_val=0, max_val=LAST_N)
                        buf = eng.snap(n % 2, min_val=0, max_val=1)
                        eng.wait_ge(s_A_sb, n + (l + 1))
                        for c in range(chunks_of(last)):
                            eng.wait_ge(s_vec_chunk, n * CHUNKS + (c + chunk_steps(c, last)))
                            for t in tiles_of(c, last):
                                for i in range(banks):
                                    done = eng.matmul(A[:, bass.ds(buf, 1), i * BANK:i * BANK + width]
                                                      .rearrange("p a n -> p (a n)"),
                                                      S[:, t, :], M[:, t, i * width:(i + 1) * width],
                                                      start=(t == 0), stop=(t == (TAIL if last else GROUP) - 1))
                            done.then_inc(s_chunk_free, chunk_steps(c, last))
                            if c == 1:
                                transpose_A(l, n)
                            if c == 3:
                                project(l, n)
                        eng.reg_add(passes, passes, 1)

                with eng.Fori(0, GROUPS - 1) as g:
                    group(g)
                group(GROUPS - 1, last=True)
                n = eng.snap(passes, min_val=0, max_val=LAST_N)
                transpose_A(l, n)
                project(l, n)

        @block.vector
        def _(eng):
            steps = [0]

            def step(ins):
                steps[0] += 1
                ins.then_inc(s_v, 1)

            def settled():
                eng.wait_ge(s_v, steps[0])

            for l in range(LAYERS):
                step(eng.memset(root_sb[l][:, :], 0.0))
            settled()
            eng.memset(eps[:, :], EPS).then_inc(s_root_zero, 1)
            eng.memset(less_one[:, :], -1.0)
            eng.memset(less_half[:, :], -0.5)
            eng.memset(zeros[:, :], 0.0)
            eng.memset(A[:, :, :], 0.0).then_inc(s_node, 1)
            eng.wait_ge(s_const, 2)
            step(eng.tensor_copy(node[:, :], node_i[:, :]))
            eng.sem_inc(s_sum, 1)

            def norm(done):
                for i, (a, b) in enumerate(PARTS):
                    if not done:
                        eng.wait_ge(s_x[i], 16)
                    else:
                        eng.wait_ge(s_acc_back[i], 16 * 2)
                        step(eng.scalar_tensor_tensor(out=xres[:, a:b, :], in0=h[:, a:b, :], scalar=0.0,
                                                      in1=xres[:, a:b, :], op0=MAX, op1=ADD))
                    settled()
                    step(eng.tensor_reduce(mean[:, a:b], xres[:, a:b, :], AX.X, ADD))
                    settled()
                    eng.tensor_scalar(mean[:, a:b], mean[:, a:b], 1.0 / D, None, MUL).then_inc(s_mean, 1)
                    if not done and i == 0:
                        group_least()
                    if not done and i == 2:
                        group_ends()
                    if i:
                        variance(done, i - 1)
                    if i > 1:
                        scaled(done, i - 2)
                    if not done and i == 3:
                        group_passes()
                variance(done, len(PARTS) - 1)
                scaled(done, len(PARTS) - 2)
                scaled(done, len(PARTS) - 1)

            def init(l, b):
                eng.wait_ge(s_root, l * BATCHES + b + 1)
                r0, r1 = b * BATCH, min(ROWS, (b + 1) * BATCH)
                eng.tensor_tensor(acc_init[:, r0:r1, :],
                                  O[:, b % 2, 0:(r1 - r0) * D].rearrange("p (r f) -> p r f", f=D),
                                  bias_sb[l][:, :].unsqueeze(1).to_broadcast([P, r1 - r0, D]), ADD)\
                   .then_inc(s_init_bias if l == LAYERS - 1 else s_init, 1)
                if l == LAYERS - 1:
                    eng.wait_ge(s_init_bias, b + 1)
                    eng.tensor_tensor(acc_init[:, r0:r1, :], acc_init[:, r0:r1, :], xres[:, r0:r1, :], ADD)\
                       .then_inc(s_init, 1)

            def variance(done, i):
                a, b = PARTS[i]
                eng.wait_ge(s_squares, len(PARTS) * done + i + 1)
                eng.tensor_reduce(var[:, a:b], squares[i % 2][:, 0:(b - a) * D].rearrange("p (r f) -> p r f", f=D),
                                  AX.X, ADD).then_inc(s_var, 1)

            def scaled(done, i):
                a, b = PARTS[i]
                eng.wait_ge(s_std, len(PARTS) * done + i + 1)
                step(eng.reciprocal(std[:, a:b], std[:, a:b]))
                settled()
                eng.scalar_tensor_tensor(out=h[:, a:b, :], in0=h[:, a:b, :], scalar=0.0,
                                         in1=wide(std[:, a:b], D), op0=MAX, op1=MUL).then_inc(s_h, 1)

            def group_least():
                eng.wait_ge(s_target, 1)
                by_group = rel[:, :].rearrange("p (g t) -> p g t", t=GROUP)
                eng.tensor_reduce(least[:, 0, :], by_group, AX.X, ALU.min).then_inc(s_tab_min, 1)
                eng.tensor_reduce(least[:, 1, :], by_group, AX.X, MAX).then_inc(s_tab_min, 1)

            def group_ends():
                eng.wait_ge(s_tab_T, 1)
                step(eng.tensor_reduce(ends[:, 0:1], A[0:GROUPS, 0, 0:P], AX.X, ALU.min))
                step(eng.tensor_reduce(ends[:, 1:2], A[0:GROUPS, 0, P:2 * P], AX.X, MAX))
                settled()
                eng.tensor_copy(ends_wide[:, :, :], ends[:, :].unsqueeze(2).to_broadcast([GROUPS, 2, P]))\
                   .then_inc(s_tab_ends, 1)

            def group_passes():
                eng.wait_ge(s_tab_wide, 1)
                eng.wait_ge(s_starts, 1)
                step(eng.tensor_copy(ends_i[0:1, :, :], A[0:1, 0, BANK:BANK + 2 * P]
                                     .rearrange("p (a g) -> p a g", a=2)[:, :, 0:GROUPS]))
                settled()
                step(eng.tensor_tensor(ends_i[0:1, 1, :], ends_i[0:1, 1, :], ends_i[0:1, 0, :], SUB))
                step(eng.tensor_copy(tab[0:1, :, 0], ends_i[0:1, 0, :]))
                settled()
                step(eng.tensor_scalar(ends_i[0:1, 1, :], ends_i[0:1, 1, :], WINDOW.bit_length() - 1, None,
                                       ALU.arith_shift_right))
                settled()
                step(eng.tensor_scalar(span[0:1, :], ends_i[0:1, 1, :], 1.0, None, ADD))
                settled()
                eng.tensor_copy(tab[0:1, :, 1], span[0:1, :]).then_inc(s_tab, 1)

            def group_coef(l, tile0):
                if LAYER_K[l] == SPLINE_K:
                    return eng.tensor_tensor(
                        coef[:, :, :].rearrange("p t (i j) -> p t i j", j=3),
                        basis[:, 0, bass.ds(tile0, GROUP), :].unsqueeze(3).to_broadcast([P, GROUP, 3, 3]),
                        basis[:, 1, bass.ds(tile0, GROUP), :].unsqueeze(2).to_broadcast([P, GROUP, 3, 3]), MUL)
                return eng.tensor_tensor(
                    coef[:, :, 0:RELATIONS],
                    relation[:, bass.ds(tile0, GROUP)].unsqueeze(2).to_broadcast([P, GROUP, RELATIONS]),
                    node[:, 0:RELATIONS].unsqueeze(1).to_broadcast([P, GROUP, RELATIONS]), ALU.is_equal)

            def flush(l, n):
                eng.wait_ge(s_O, n + (l + 2))
                eng.wait_ge(s_acc_load, n * 16 + 16)
                eng.tensor_tensor(acc_sum[:, :], O[:, 0, 0:D], acc_in[:, :], ADD).then_inc(s_sum, 1)

            passes = counter(eng, "vector_passes")
            for l in range(LAYERS):
                if l == 0:
                    norm(0)
                    eng.wait_ge(s_edges[0], 48)
                    for place in range(RING):
                        eng.tensor_copy(index[:, place, :], srcs[:, place * GROUP:(place + 1) * GROUP])\
                           .then_inc(s_index, 1)
                    eng.wait_ge(s_weights, 16 * sum(4 + (k * D % P > 0) for k in LAYER_K))
                if l == 2:
                    norm(1)
                if l:
                    eng.wait_ge(s_acc_init, 16 * l)
                for b in range(BATCHES):
                    init(l, b)
                if l == 0:
                    eng.wait_ge(s_basis, 4)
                ks = LAYER_K[l]

                def group(g, place, trip, last=False):
                    count = eng.value_load(tab[0:1, bass.ds(g, 1), 1:2].rearrange("p a b -> p (a b)"),
                                           min_val=1, max_val=MAX_PASSES)
                    tile0 = g * GROUP if isinstance(g, int) else eng.snap(g * GROUP, min_val=0, max_val=TILES - GROUP)
                    n = eng.snap(passes, min_val=0, max_val=LAST_N)
                    eng.wait_ge(s_rel, n + g + (l * GROUPS + 1))
                    eng.tensor_copy(relq[:, :], rel[:, bass.ds(tile0, GROUP)]).then_inc(s_rel, 1)
                    group_coef(l, tile0).then_inc(s_coef, 1)
                    with eng.Fori(0, count):
                        n = eng.snap(passes, min_val=0, max_val=LAST_N)
                        eng.wait_ge(s_rel, n + g + (l * GROUPS + 2))
                        eng.wait_ge(s_coef, g + (l * GROUPS + 1))
                        for c in range(chunks_of(last)):
                            tiles = tiles_of(c, last)
                            t0, t1 = tiles[0], tiles[-1] + 1
                            eng.wait_ge(s_chunk_free, n * CHUNKS + (c + 1))
                            eng.tensor_tensor(S[:, t0:t1, :],
                                              node[:, :].unsqueeze(1).to_broadcast([P, t1 - t0, WINDOW]),
                                              relq[:, t0:t1].unsqueeze(2).to_broadcast([P, t1 - t0, WINDOW]),
                                              ALU.is_equal)
                            eng.wait_ge(s_gathered[place][c], gathered(l, place, c, trip, last))
                            for t in tiles:
                                done = eng.scalar_tensor_tensor(
                                    out=M[:, t, 0:ks * D].rearrange("p (k f) -> p k f", f=D),
                                    in0=rows[:, place, t:t + 1, :].to_broadcast([P, ks, D]), scalar=0.0,
                                    in1=coef[:, t, 0:ks].unsqueeze(2).to_broadcast([P, ks, D]),
                                    op0=MAX, op1=MUL)
                            done.then_inc(s_vec_chunk, chunk_steps(c, last))
                        flush(l, n)
                        eng.wait_ge(s_vec_chunk, n * CHUNKS + CHUNKS)
                        eng.tensor_scalar(relq[:, :], relq[:, :], float(WINDOW), None, SUB).then_inc(s_rel, 1)
                        eng.reg_add(passes, passes, 1)
                    n = eng.snap(passes, min_val=0, max_val=LAST_N)
                    eng.wait_ge(s_vec_chunk, n * CHUNKS)
                    eng.tensor_copy(index[:, place, :], srcs[:, bass.ds(tile0 + RING * GROUP, GROUP)])\
                       .then_inc(s_index, 1)

                with eng.Fori(0, TRIPS) as trip:
                    for place in range(RING):
                        group(eng.snap(trip * RING + place, min_val=0, max_val=GROUPS - 2), place, trip)
                group(GROUPS - 1, 0, TRIPS, last=True)
                n = eng.snap(passes, min_val=0, max_val=LAST_N)
                flush(l, n)
    return nc


def kernel(**inputs):
    import numpy as np
    import concourse.bacc as bacc
    from concourse.bass_utils import run_bass_kernel_spmd

    def by_tile(a, fill):
        a = np.asarray(a)
        up = np.full((TILES * P,) + a.shape[1:], fill, a.dtype)
        up[:EDGES] = a
        return np.ascontiguousarray(np.moveaxis(up.reshape((TILES, P) + a.shape[1:]), 1, 0))

    x = np.zeros((NODES_UP, D), np.asarray(inputs["x"]).dtype)
    x[:NODES] = inputs["x"]
    arrays = {
        "x": x,
        "src": by_tile(inputs["src"], 0),
        "dst": by_tile(inputs["dst"], NODES),
        "attr": np.ascontiguousarray(np.moveaxis(by_tile(inputs["edge_attr_2"], 0), 2, 1)),
        "etype": by_tile(inputs["edge_type_8"], 0),
    }
    for part in ("L0", "L1"):
        for n in ("1", "2"):
            w = np.asarray(inputs[f"{part}_gnn_W{n}"])
            arrays[f"W_{part}_{n}"] = np.ascontiguousarray(w.reshape(-1, D))
            arrays[f"root_{part}_{n}"] = np.ascontiguousarray(inputs[f"{part}_gnn_root{n}"])
            arrays[f"b_{part}_{n}"] = np.ascontiguousarray(inputs[f"{part}_gnn_b{n}"])

    nc = bacc.Bacc("TRN2", target_bir_lowering=False, num_devices=1)
    aps = {name: nc.dram_tensor(name, a.shape, mybir.dt.from_np(a.dtype), kind="ExternalInput").ap()
           for name, a in arrays.items()}
    out = nc.dram_tensor("out", (ACC_ROWS, D), FP32, kind="ExternalOutput").ap()
    layers = [f"{part}_{n}" for part in ("L0", "L1") for n in ("1", "2")]
    gnn_kernel(nc, aps["x"], aps["src"], aps["dst"], aps["attr"], aps["etype"],
               [aps["W_" + s] for s in layers], [aps["root_" + s] for s in layers],
               [aps["b_" + s] for s in layers], out)
    got = run_bass_kernel_spmd(nc, [arrays], core_ids=[0])
    return got.results[0]["out"][:NODES]
```
